# Optimizing a Trainium2 kernel written in Bass

```python
import numpy as np
import jax
import jax.numpy as jnp

def _softmax(x, axis=-1):
    return jax.nn.softmax(x, axis=axis)

def _gelu(x):
    return jax.nn.gelu(x, approximate=True)

def _silu(x):
    return jax.nn.silu(x)

def _sigmoid(x):
    return jax.nn.sigmoid(x)

def _layernorm(x, axis=-1, eps=1e-05):
    m = jnp.mean(x, axis=axis, keepdims=True)
    v = jnp.var(x, axis=axis, keepdims=True)
    return (x - m) / jnp.sqrt(v + eps)

def _scatter_add(tgt, idx, src, axis=0):
    return tgt.at[idx].add(src)

def _segment_sum(src, seg, n):
    return jax.ops.segment_sum(src, seg, n)
kernel_name = 'mk_adaln_ffn_d1_seqx_r2_f89b1b'

def setup_inputs(seed: int=0):
    np.random.seed(seed)
    _w = jnp.asarray

    def _rec_inputs():
        import jax
        import jax.numpy as jnp
        _rk = jax.random.key(seed)
        x = -7.109e-05 + 0.9999 * jax.random.normal(jax.random.fold_in(_rk, 1), (8, 1024, 512), jnp.float32)
        _lenS = 1024 - jax.random.randint(jax.random.fold_in(_rk, 7), (8,), 0, max(1, 1024 // 4) + 1, jnp.int32)
        _lenS2 = 1024 - jax.random.randint(jax.random.fold_in(_rk, 8), (8,), 0, max(1, 1024 // 4) + 1, jnp.int32)
        cond_512 = 0.0061147 + 1.02565 * jax.random.normal(jax.random.fold_in(_rk, 11), (8, 256), jnp.float32)
        return (x, cond_512)
    x, cond_512 = _rec_inputs()

    def _L0_cond_setup():
        import jax, jax.numpy as jnp
        import numpy as np
        W_DIM = 256
        CLAMP = 256.0
        key = jax.random.key(seed)
        ks = jax.random.split(key, 6)
        B, L, C = (8, 4096, 512)
        return {'x': jax.random.normal(ks[0], (B, L, C), dtype=jnp.float32), 'w': jax.random.normal(ks[1], (B, W_DIM), dtype=jnp.float32), 'weight': jax.random.normal(ks[2], (C, C), dtype=jnp.float32), 'bias': jax.random.normal(ks[3], (C,), dtype=jnp.float32), 'affine_w': jax.random.normal(ks[4], (C, W_DIM), dtype=jnp.float32), 'affine_b': jnp.ones((C,), dtype=jnp.float32)}
    _L0_cond_all = _L0_cond_setup()
    _L0_cond_in = {k: v for k, v in _L0_cond_all.items() if k in ('weight', 'bias', 'affine_w', 'affine_b')}
    del _L0_cond_all

    def _L0_ffn_setup():
        import jax, jax.numpy as jnp
        import numpy as np
        B, T, C = (1, 2048, 512)
        E, K = (64, 8)
        G, TG = (8, 4)
        H, HS = (256, 1024)
        STD = 0.02

        def _route(xf, router_w, e_bias):
            S = xf.shape[0]
            scores = jax.nn.sigmoid(xf @ router_w.T)
            sb = scores + e_bias
            epg = E // G
            grp = jax.lax.top_k(sb.reshape(S, G, epg), K // TG)[0].sum(-1)
            gidx = jax.lax.top_k(grp, TG)[1]
            gmask = jnp.zeros((S, G), bool).at[jnp.arange(S)[:, None], gidx].set(True)
            emask = jnp.repeat(gmask, epg, axis=1)
            masked = jnp.where(emask, sb, -jnp.inf)
            topk_idx = jax.lax.top_k(masked, K)[1]
            w = jnp.take_along_axis(scores, topk_idx, axis=1)
            w = w / (w.sum(-1, keepdims=True) + 1e-20)
            return (topk_idx, w)
        key = jax.random.key(seed)
        ks = jax.random.split(key, 9)
        return {'x': jax.random.normal(ks[0], (B, T, C), jnp.float32), 'router_w': jax.random.normal(ks[1], (E, C), jnp.float32) * C ** (-0.5), 'e_bias': jnp.zeros((E,), jnp.float32), 'gate_w': jax.random.normal(ks[2], (E, C, H), jnp.float32) * STD, 'up_w': jax.random.normal(ks[3], (E, C, H), jnp.float32) * STD, 'down_w': jax.random.normal(ks[4], (E, H, C), jnp.float32) * STD, 'sh_gate_w': jax.random.normal(ks[5], (C, HS), jnp.float32) * STD, 'sh_up_w': jax.random.normal(ks[6], (C, HS), jnp.float32) * STD, 'sh_down_w': jax.random.normal(ks[7], (HS, C), jnp.float32) * STD}
    _L0_ffn_all = _L0_ffn_setup()
    _L0_ffn_in = {k: v for k, v in _L0_ffn_all.items() if k in ('router_w', 'e_bias', 'gate_w', 'up_w', 'down_w', 'sh_gate_w', 'sh_up_w', 'sh_down_w')}
    del _L0_ffn_all
    return {'x': x, 'cond_512': cond_512, 'L0_cond_weight': _L0_cond_in['weight'], 'L0_cond_bias': _L0_cond_in['bias'], 'L0_cond_affine_w': _L0_cond_in['affine_w'], 'L0_cond_affine_b': _L0_cond_in['affine_b'], 'L0_ffn_router_w': _L0_ffn_in['router_w'], 'L0_ffn_e_bias': _L0_ffn_in['e_bias'], 'L0_ffn_gate_w': _L0_ffn_in['gate_w'], 'L0_ffn_up_w': _L0_ffn_in['up_w'], 'L0_ffn_down_w': _L0_ffn_in['down_w'], 'L0_ffn_sh_gate_w': _L0_ffn_in['sh_gate_w'], 'L0_ffn_sh_up_w': _L0_ffn_in['sh_up_w'], 'L0_ffn_sh_down_w': _L0_ffn_in['sh_down_w']}

def reference(x, cond_512, L0_cond_weight, L0_cond_bias, L0_cond_affine_w, L0_cond_affine_b, L0_ffn_router_w, L0_ffn_e_bias, L0_ffn_gate_w, L0_ffn_up_w, L0_ffn_down_w, L0_ffn_sh_gate_w, L0_ffn_sh_up_w, L0_ffn_sh_down_w):
    import jax
    import jax.numpy as jnp

    def _L0_cond_ref(x, w, weight, bias, affine_w, affine_b):
        import jax, jax.numpy as jnp
        import numpy as np
        W_DIM = 256
        CLAMP = 256.0
        B, L, C = x.shape
        gain = 1.0 / np.sqrt(W_DIM).astype(np.float32)
        styles = w @ (affine_w * gain).T + affine_b
        ws = weight[None, :, :] * styles[:, None, :]
        dcoefs = jax.lax.rsqrt(jnp.sum(ws * ws, axis=2) + 1e-08)
        xm = x * styles[:, None, :]
        y = jnp.einsum('blc,oc->blo', xm, weight)
        y = y * dcoefs[:, None, :]
        y = jnp.clip(y + bias, -CLAMP, CLAMP)
        return y

    def _L0_ffn_ref(x, router_w, e_bias, gate_w, up_w, down_w, sh_gate_w, sh_up_w, sh_down_w):
        import jax, jax.numpy as jnp
        import numpy as np
        B, T, C = (1, 2048, 512)
        E, K = (64, 8)
        G, TG = (8, 4)
        H, HS = (256, 1024)
        STD = 0.02

        def _route(xf, router_w, e_bias):
            S = xf.shape[0]
            scores = jax.nn.sigmoid(xf @ router_w.T)
            sb = scores + e_bias
            epg = E // G
            grp = jax.lax.top_k(sb.reshape(S, G, epg), K // TG)[0].sum(-1)
            gidx = jax.lax.top_k(grp, TG)[1]
            gmask = jnp.zeros((S, G), bool).at[jnp.arange(S)[:, None], gidx].set(True)
            emask = jnp.repeat(gmask, epg, axis=1)
            masked = jnp.where(emask, sb, -jnp.inf)
            topk_idx = jax.lax.top_k(masked, K)[1]
            w = jnp.take_along_axis(scores, topk_idx, axis=1)
            w = w / (w.sum(-1, keepdims=True) + 1e-20)
            return (topk_idx, w)
        Bq, Tq, Cq = x.shape
        xf = x.reshape(Bq * Tq, Cq)
        shared = jax.nn.silu(xf @ sh_gate_w) * (xf @ sh_up_w) @ sh_down_w
        topk_idx, w = _route(xf, router_w, e_bias)
        fe = topk_idx.reshape(-1)
        order = jnp.argsort(fe, stable=True)
        tok = order // K
        sorted_x = xf[tok]
        group_sizes = jnp.bincount(fe, length=E).astype(jnp.int32)
        g = jax.lax.ragged_dot(sorted_x, gate_w, group_sizes)
        u = jax.lax.ragged_dot(sorted_x, up_w, group_sizes)
        h = jax.nn.silu(g) * u
        o = jax.lax.ragged_dot(h, down_w, group_sizes)
        o = o * w.reshape(-1)[order][:, None]
        routed = jnp.zeros_like(xf).at[tok].add(o)
        return (shared + routed).reshape(Bq, Tq, Cq)
    x = x + _L0_ffn_ref(_L0_cond_ref(x, cond_512, L0_cond_weight, L0_cond_bias, L0_cond_affine_w, L0_cond_affine_b), L0_ffn_router_w, L0_ffn_e_bias, L0_ffn_gate_w, L0_ffn_up_w, L0_ffn_down_w, L0_ffn_sh_gate_w, L0_ffn_sh_up_w, L0_ffn_sh_down_w)
    return x

_drawn_inputs = setup_inputs


def setup_inputs(seed=0):
    import zlib

    import numpy as np

    out = dict(_drawn_inputs(seed))
    spreads = {'L0_cond_affine_b': (1.0, 0.6), 'L0_ffn_e_bias': (0.0, 1.361)}
    factors = {'L0_ffn_router_w': 3.278}
    for name, (base, spread) in spreads.items():
        noise = np.random.default_rng([zlib.crc32(name.encode()), seed]).standard_normal(out[name].shape)
        drawn = base * np.exp(spread * noise) if base else spread * noise
        out[name] = jnp.asarray(drawn.astype(out[name].dtype))
    for name, factor in factors.items():
        out[name] = (out[name] * factor).astype(out[name].dtype)
    return out
```

```python
from contextlib import ExitStack

import concourse.bass as bass
from concourse import mybir

ALU = mybir.AluOpType
ACT = mybir.ActivationFunctionType
AX_X = mybir.AxisListType.X
F32 = mybir.dt.float32
F32R = mybir.dt.float32r
BF16 = mybir.dt.bfloat16
I32 = mybir.dt.int32
U32 = mybir.dt.uint32

P = 128

NEG = -3.0e38
TAKEN = -3.3e38


def some(n):
    return not isinstance(n, int) or n > 0


def sub_exact(nc, out, full, high):
    return nc.vector.tensor_tensor(out, full, high.bitcast(F32), ALU.subtract)


def build(nc, x, cond, cw, cbias, aff_w, aff_b, router_w, e_bias, gate_w, up_w, down_w,
          sh_gate, sh_up, sh_down, out):
    B, L, C = x.shape
    N = B * L
    WD = cond.shape[1]
    E, _, H = gate_w.shape
    HS = sh_gate.shape[1]
    TOPK, GROUPS, TOPG = 8, 8, 4
    EPG = E // GROUPS
    CLAMP = 256.0
    KC = C // P
    KH = H // P
    KW = WD // P
    TB = 512
    TT = TB // P
    NBLK = N // TB
    NCH = HS // P
    LOG_P = P.bit_length() - 1
    MAXT = N * TOPK // P + E
    UN = 4
    TQ = -(-(MAXT + 2 * UN) // P)
    REG = N
    LROWS = -(-(E * REG + TQ * P * P) // (P * P)) * P * P
    FLD = 8

    xf = x.rearrange("b l c -> (b l) c")
    of = out.rearrange("b l c -> (b l) c")
    y_rows = nc.dram_tensor("y_rows", (N + P, C), F32).ap()
    acc = nc.dram_tensor("acc_rows", (N + P, C), F32).ap()
    slots = nc.dram_tensor("slot_list", (LROWS, 2), I32).ap()
    table = nc.dram_tensor("tile_table", (TQ * P, FLD), I32).ap()

    top = ExitStack()

    def sem(name):
        return top.enter_context(nc.semaphore(name))

    with top:
        keep = ExitStack()
        top.enter_context(keep)

        def sb_in(stack):
            return lambda name, shape, dt=F32: stack.enter_context(nc.sbuf_tensor(name, shape, dt))

        bank = [top.enter_context(nc.psum_tensor(f"bank{n}", [P, 512], F32)) for n in range(8)]

        sb = sb_in(keep)
        ident = sb("ident", [P, P])
        base = sb("base", [P, E])
        base0 = sb("base0", [P, E])
        zrow = sb("zrow", [P, C])

        dense = ExitStack()
        sb = sb_in(dense)
        sgw = [sb("sh_gate_h", [P, KC, HS], F32R), sb("sh_gate_l", [P, KC, HS], F32R)]
        suw = [sb("sh_up_h", [P, KC, HS], F32R), sb("sh_up_l", [P, KC, HS], F32R)]
        sdw = [sb("sh_down_h", [P, NCH, C], F32R), sb("sh_down_l", [P, NCH, C], F32R)]
        wt = [sb("w_h", [P, KC, C], F32R), sb("w_l", [P, KC, C], F32R)]
        rt = sb("router_t", [P, KC, E])
        bias_c = sb("bias_c", [P, KC])
        styles = sb("styles", [P, NBLK, 2 * KC])
        eb = sb("e_bias_b", [P, E])
        before = sb("before", [P, P], BF16)
        ones = sb("ones", [P, P], BF16)
        iota_e = sb("iota_e", [P, E])
        lower = sb("lower", [P, GROUPS, GROUPS])
        tok = sb("tok", [P, TT], I32)

        with ExitStack() as tmp:
            sb = sb_in(tmp)
            stage = [sb("stage_g", [P, KC, HS]), sb("stage_u", [P, KC, HS]), sb("stage_d", [P, NCH, C])]
            w_raw = sb("w_raw", [P, KC, C])
            aw_raw = sb("aw_raw", [P, KC, WD])
            rw_raw = sb("rw_raw", [E, C])
            cond_raw = sb("cond_raw", [B, WD])
            ab = sb("ab", [P, KC])
            cond_t = sb("cond_t", [P, KW, B])
            aw_t = sb("aw_t", [P, KW, C])
            w_sq = sb("w_sq", [P, KC, C])
            st = sb("st", [P, KC, B])
            st_sq = sb("st_sq", [P, KC, B])
            dco = sb("dco", [P, KC, B])
            sq_sum = sb("sq_sum", [P, KC, B])
            root = sb("root", [P, KC, B])
            pad = sb("pad", [P, P, 2], I32)
            iota_i = sb("iota_i", [P, E], I32)
            low_i = sb("low_i", [P, GROUPS, GROUPS], I32)

            ld_small, ld_w, ld_aff, ld_r = sem("ld_small"), sem("ld_w"), sem("ld_aff"), sem("ld_r")
            ld_sh = [sem("ld_sh_gate"), sem("ld_sh_up"), sem("ld_sh_down")]
            made = sem("made")
            zeroed = sem("zeroed")
            filled = sem("filled")
            turned = sem("turned")
            copied = sem("copied")
            squared = sem("squared")
            high = sem("high")
            low = sem("low")
            st_mm, st_ok, sq_mm = sem("st_mm"), sem("st_ok"), sem("sq_mm")
            chain = sem("setup_chain")
            rooted = sem("rooted")
            ROOT_AT = 6
            blk = tmp.enter_context(nc.Block())

            @blk.sync
            def _(sp):
                sp.dma_start(aw_raw[:], aff_w.rearrange("(k p) w -> p k w", p=P)).then_inc(ld_aff, 16)
                sp.dma_start(cond_raw[:], cond).then_inc(ld_aff, 16)
                sp.dma_start(w_raw[:], cw.rearrange("(k p) c -> p k c", p=P)).then_inc(ld_w, 16)
                sp.dma_start(rw_raw[:], router_w).then_inc(ld_r, 16)
                with nc.allow_non_contiguous_dma(reason="small columns"):
                    sp.dma_start(ab[:], aff_b.rearrange("(k p) -> p k", p=P)).then_inc(ld_small, 16)
                    sp.dma_start(bias_c[:], cbias.rearrange("(k p) -> p k", p=P)).then_inc(ld_small, 16)
                sp.dma_start(eb[:], e_bias.partition_broadcast(P)).then_inc(ld_small, 16)
                for n, w in enumerate((sh_gate, sh_up, sh_down)):
                    sp.dma_start(stage[n][:], w.rearrange("(k p) h -> p k h", p=P)).then_inc(ld_sh[n], 16)
                sp.wait_ge(made, 7)
                per = LROWS // P // P
                sp.dma_start(slots.rearrange("(q a r) k -> q a (r k)", q=P, a=per),
                             pad[:].rearrange("p r k -> p (r k)").unsqueeze(1).to_broadcast([P, per, 2 * P])
                             ).then_inc(filled, 16)
                sp.wait_ge(zeroed, 1)
                sp.dma_start(y_rows[N:N + P, :], zrow[:]).then_inc(filled, 16)
                sp.dma_start(acc[N:N + P, :], zrow[:]).then_inc(filled, 16)
                sp.wait_ge(filled, 48)

            @blk.gpsimd
            def _(pool):
                nc.gpsimd.memset(ident[:], 0.0).then_inc(made, 1)
                pool.wait_ge(made, 1)
                nc.gpsimd.affine_select(out=ident[:], in_=ident[:], compare_op=ALU.not_equal, fill=1.0,
                                        base=0, pattern=[[-1, P]], channel_multiplier=1).then_inc(made, 1)
                nc.gpsimd.memset(ones[:], 1.0).then_inc(made, 1)
                pool.wait_ge(made, 3)
                nc.gpsimd.affine_select(out=before[:], in_=ones[:], compare_op=ALU.is_gt, fill=0.0,
                                        base=0, pattern=[[1, P]], channel_multiplier=-1).then_inc(made, 1)
                nc.gpsimd.memset(pad[:], 0).then_inc(made, 1)
                nc.gpsimd.iota(iota_i[:], pattern=[[1, E]], base=0, channel_multiplier=0).then_inc(made, 1)
                pool.wait_ge(made, 6)
                nc.gpsimd.iota(pad[:, :, 0:1].rearrange("p r k -> p (r k)"), pattern=[[1, P]], base=N,
                               channel_multiplier=0).then_inc(made, 1)
                nc.gpsimd.iota(low_i[:], pattern=[[1, GROUPS], [-1, GROUPS]], base=0,
                               channel_multiplier=0).then_inc(made, 1)
                nc.gpsimd.iota(tok[:], pattern=[[P, TT]], base=0, channel_multiplier=1).then_inc(made, 1)

            @blk.tensor
            def _(pe):
                pe.wait_ge(made, 2)
                pe.wait_ge(ld_aff, 32)
                for k in range(KW):
                    nc.tensor.transpose(bank[0][:, k * B:(k + 1) * B], cond_raw[:, k * P:(k + 1) * P], ident[0:B, 0:B])
                for k in range(KW):
                    for m in range(KC):
                        last = nc.tensor.transpose(bank[1 + k][:, m * P:(m + 1) * P], aw_raw[:, m, k * P:(k + 1) * P], ident[:])
                last.then_inc(turned, 1)
                pe.wait_ge(ld_r, 16)
                for k in range(KC):
                    last = nc.tensor.transpose(bank[3][:, k * E:(k + 1) * E], rw_raw[:, k * P:(k + 1) * P], ident[0:E, 0:E])
                last.then_inc(turned, 1)
                pe.wait_ge(ld_w, 16)
                for k in range(KC):
                    for m in range(KC):
                        last = nc.tensor.transpose(bank[4 + k][:, m * P:(m + 1) * P], w_raw[:, m, k * P:(k + 1) * P], ident[:])
                    last.then_inc(turned, 1)
                pe.wait_ge(copied, 2)
                for m in range(KC):
                    for k in range(KW):
                        last = nc.tensor.matmul(bank[0][:, 64 + m * B:64 + (m + 1) * B], aw_t[:, k, m * P:(m + 1) * P],
                                                cond_t[:, k, :], start=(k == 0), stop=(k == KW - 1))
                last.then_inc(st_mm, 1)
                pe.wait_ge(st_ok, 1)
                pe.wait_ge(squared, KC)
                for m in range(KC):
                    for k in range(KC):
                        last = nc.tensor.matmul(bank[1][:, m * B:(m + 1) * B], w_sq[:, k, m * P:(m + 1) * P],
                                                st_sq[:, k, :], start=(k == 0), stop=(k == KC - 1))
                last.then_inc(sq_mm, 1)

            @blk.scalar
            def _(act):
                for k in range(KC):
                    act.wait_ge(turned, 3 + k)
                    nc.scalar.copy(wt[0][:, k, :], bank[4 + k][:]).then_inc(high, 1)
                    nc.scalar.activation(w_sq[:, k, :], bank[4 + k][:], ACT.Square).then_inc(squared, 1)
                for n, (w, s) in enumerate(((sgw, stage[0]), (suw, stage[1]), (sdw, stage[2]))):
                    act.wait_ge(ld_sh[n], 16)
                    nc.scalar.copy(w[0][:], s[:]).then_inc(high, 1)
                act.wait_ge(chain, ROOT_AT)
                nc.scalar.activation(root[:], sq_sum[:], ACT.Sqrt).then_inc(rooted, 1)

            @blk.vector
            def _(dve):
                n_link = [0]

                def link(ins):
                    n_link[0] += 1
                    ins.then_inc(chain, 1)
                    dve.wait_ge(chain, n_link[0])

                nc.vector.memset(zrow[:], 0.0).then_inc(zeroed, 1)
                dve.wait_ge(made, 9)
                link(nc.vector.tensor_copy(iota_e[:], iota_i[:]))
                link(nc.vector.tensor_scalar(base[:], iota_e[:], float(REG), None, ALU.mult))
                link(nc.vector.tensor_copy(base0[:], base[:]))
                link(nc.vector.tensor_scalar(lower[:], low_i[:], 0.0, None, ALU.is_gt))
                dve.wait_ge(turned, 1)
                nc.vector.tensor_copy(cond_t[:].rearrange("p k b -> p (k b)"), bank[0][:, 0:KW * B])
                for k in range(KW):
                    last = nc.vector.tensor_copy(aw_t[:, k, :], bank[1 + k][:])
                    if k == KW - 1:
                        last.then_inc(copied, 1)
                dve.wait_ge(turned, 2)
                nc.vector.tensor_copy(rt[:].rearrange("p k e -> p (k e)"), bank[3][:, 0:KC * E]).then_inc(copied, 1)
                dve.wait_ge(st_mm, 1)
                dve.wait_ge(ld_small, 48)
                gain = float(WD) ** -0.5
                for m in range(KC):
                    last = nc.vector.tensor_scalar(st[:, m, :], bank[0][:, 64 + m * B:64 + (m + 1) * B], gain, ab[:, m:m + 1],
                                                   ALU.mult, ALU.add)
                link(last)
                nc.vector.tensor_tensor(st_sq[:], st[:], st[:], ALU.mult).then_inc(st_ok, 1)
                for k in range(KC):
                    dve.wait_ge(squared, k + 1)
                    sub_exact(nc, wt[1][:, k, :], bank[4 + k][:], wt[0][:, k, :])
                dve.wait_ge(sq_mm, 1)
                flat_d = "p k b -> p (k b)"
                link(nc.vector.tensor_scalar(sq_sum[:].rearrange(flat_d), bank[1][:, 0:KC * B], 1e-8, None, ALU.add))
                dve.wait_ge(rooted, 1)
                link(nc.vector.reciprocal(dco[:], root[:]))
                link(nc.vector.tensor_tensor(root[:], dco[:], dco[:], ALU.mult))
                link(nc.vector.tensor_tensor(root[:], root[:], sq_sum[:], ALU.mult))
                link(nc.vector.tensor_scalar(root[:], root[:], -0.5, 1.5, ALU.mult, ALU.add))
                link(nc.vector.tensor_tensor(dco[:], dco[:], root[:], ALU.mult))
                per = NBLK // B
                for h in range(per):
                    v = styles[:].rearrange("p (b h) k -> p h k b", h=per)[:, h]
                    nc.vector.tensor_copy(v[:, 0:KC, :], st[:])
                    link(nc.vector.tensor_copy(v[:, KC:2 * KC, :], dco[:]))
                for n, (w, s) in enumerate(((sgw, stage[0]), (suw, stage[1]), (sdw, stage[2]))):
                    dve.wait_ge(high, KC + 1 + n)
                    link(sub_exact(nc, w[1][:], s[:], w[0][:]))

        with ExitStack() as tmp:
            sb = sb_in(tmp)
            xin = sb("xin", [P, TT, C])
            xres = sb("xres", [P, TT, C])
            xt = [sb("xt_h", [P, KC, TB], F32R), sb("xt_l", [P, KC, TB], F32R)]
            yt = sb("yt", [P, KC, TB])
            yp = [sb("y_h", [P, KC, TB], F32R), sb("y_l", [P, KC, TB], F32R)]
            yrow = sb("yrow", [P, 2, C])
            cur = sb("cur", [P, 2 * KC])
            sg = sb("sg", [P, TB])
            hf = sb("hf", [P, 2, TB])
            hp = [sb("h_h", [P, 2, TB], F32R), sb("h_l", [P, 2, TB], F32R)]
            sc = sb("sc", [P, TT, E])
            sbi = sb("sbi", [P, TT, E])
            t1 = sb("t1", [P, TT, E])
            t2 = sb("t2", [P, TT, E])
            mask = sb("mask", [P, TT, E], BF16)
            wn = sb("wn", [P, TT, E])
            sl = sb("sl", [P, TT, E])
            g1, g2, g3 = (sb(f"g{n}", [P, TT, GROUPS]) for n in range(3))
            v8 = sb("v8", [P, TT, TOPK])
            i8 = sb("i8", [P, TT, TOPK], U32)
            i8f = sb("i8f", [P, TT, TOPK])
            pf = sb("pf", [P, TT, TOPK])
            pos = sb("pos", [P, TT, TOPK], U32)
            ent = sb("ent", [P, TT, TOPK, 2], I32)
            den = sb("den", [P, TT])
            rden = sb("rden", [P, TT])
            oh = sb("oh", [P, TOPK, E])
            oh2 = sb("oh2", [P, TOPK, E])

            bg, bu = bank[0], bank[1]
            bo = bank[2:6]
            misc = bank[6:8]

            x_ld, xres_ld, o_st = sem("x_ld"), sem("xres_ld"), sem("o_st")
            y_st = [sem("y_st0"), sem("y_st1")]
            pe_tx, act_xth, dve_xtl = sem("pe_tx"), sem("act_xth"), sem("dve_xtl")
            pe_y, act_y, dve_y = sem("pe_y"), sem("act_y"), sem("dve_y")
            pe_ty, act_yrow = sem("pe_ty"), sem("act_yrow")
            act_yh, dve_yl = sem("act_yh"), sem("dve_yl")
            pe_lg, act_sc, dve_sc = sem("pe_lg"), sem("act_sc"), sem("dve_sc")
            pe_g, act_sg, pe_u, dve_h = sem("pe_g"), sem("act_sg"), sem("pe_u"), sem("dve_h")
            act_hh, dve_hl, pe_d, dve_o = sem("act_hh"), sem("dve_hl"), sem("pe_d"), sem("dve_o")
            dve_cur, dve_mask, pe_rank, dve_rank = sem("dve_cur"), sem("dve_mask"), sem("pe_rank"), sem("dve_rank")
            dve_ent, scattered = sem("dve_ent"), sem("scattered")
            steps = sem("route_steps")
            blk = tmp.enter_context(nc.Block())

            def rows(ap, q, t=None):
                if t is None:
                    return ap[bass.ds(q * TB, TB), :].rearrange("(t p) c -> p t c", p=P)
                return ap[bass.ds(q * TB + t * P, P), :]

            @blk.sync
            def _(sp):
                def load_x(q):
                    sp.dma_start(xin[:], rows(xf, q)).then_inc(x_ld, 16)

                def store_y(q):
                    for t in range(TT):
                        sp.wait_ge(act_yrow, TT * q + t + 1)
                        sp.dma_start(rows(y_rows, q, t), yrow[:, t % 2, :]).then_inc(y_st[t % 2], 16)

                def body(i, prep, more):
                    if some(16 * i):
                        sp.wait_ge(o_st, 16 * i)
                    sp.dma_start(xres[:], rows(xf, i)).then_inc(xres_ld, 16)
                    if prep:
                        store_y(i + 1)
                    if more:
                        sp.wait_ge(pe_tx, KC * (i + 2))
                        load_x(i + 2)
                    sp.wait_ge(dve_o, TT * (i + 1))
                    sp.dma_start(rows(acc, i), xres[:]).then_inc(o_st, 16)

                load_x(0)
                store_y(0)
                sp.wait_ge(pe_tx, KC)
                load_x(1)
                body(0, True, True)
                with sp.Fori(1, NBLK - 2) as i:
                    body(i, True, True)
                body(NBLK - 2, True, False)
                body(NBLK - 1, False, False)
                sp.wait_ge(o_st, 16 * NBLK)
                for q in range(2):
                    sp.wait_ge(y_st[q], 16 * NBLK * TT // 2)

            @blk.gpsimd
            def _(pool):
                def body(i):
                    for t in range(TT):
                        pool.wait_ge(dve_ent, TT * i + t + 1)
                        pool.nop(nofuse=True)
                        for k in range(TOPK):
                            nc.gpsimd.indirect_dma_start(
                                slots, bass.IndirectOffsetOnAxis(ap=pos[:, t, k:k + 1], axis=0),
                                ent[:, t, k, :], None).then_inc(scattered, 16)

                with pool.Fori(0, NBLK) as i:
                    body(i)
                pool.wait_ge(scattered, 16 * TOPK * TT * NBLK)

            @blk.tensor
            def _(pe):
                def products(dst, lhs, rhs, chunks, start=True, stop=True):
                    n = 0
                    for k in chunks:
                        for a, b in ((0, 0), (0, 1), (1, 0)):
                            last = nc.tensor.matmul(dst, lhs(a, k), rhs(b, k), start=start and n == 0,
                                                    stop=stop and n == 3 * len(chunks) - 1)
                            n += 1
                    return last

                def turn_x(q, k, first):
                    if k == 0:
                        pe.wait_ge(x_ld, 16 * (q + 1))
                        if not first:
                            if some(TT * q):
                                pe.wait_ge(act_yrow, TT * q)
                    elif k == 1:
                        if not first:
                            if some(q):
                                pe.wait_ge(act_sc, q)
                    else:
                        pe.wait_ge(dve_xtl, KC * q + k - 1)
                    for t in range(TT):
                        last = nc.tensor.transpose(misc[k % 2][:, t * P:(t + 1) * P], xin[:, t, k * P:(k + 1) * P], ident[:])
                    last.then_inc(pe_tx, 1)

                def make_y(q, m, first):
                    if m == 0:
                        pe.wait_ge(dve_xtl, KC * (q + 1))
                    elif m == 1:
                        if not first:
                            if some(q):
                                pe.wait_ge(dve_rank, q)
                    else:
                        pe.wait_ge(act_y, KC * q + m - 1)
                    products(misc[(m + 1) % 2][:], lambda a, k: wt[a][:, k, m * P:(m + 1) * P],
                             lambda b, k: xt[b][:, k, :], range(KC)).then_inc(pe_y, 1)

                def turn_y(q, t):
                    if t == 0:
                        pe.wait_ge(dve_y, KC * (q + 1))
                    elif t >= 2:
                        pe.wait_ge(act_yrow, TT * q + t - 1)
                    for k in range(KC):
                        last = nc.tensor.transpose(misc[(t + 1) % 2][:, k * P:(k + 1) * P], yt[:, k, t * P:(t + 1) * P], ident[:])
                    last.then_inc(pe_ty, 1)

                def route(q):
                    pe.wait_ge(act_yrow, TT * q + 3)
                    for t in range(TT):
                        for k in range(KC):
                            last = nc.tensor.matmul(misc[1][:, t * E:(t + 1) * E], yt[:, k, t * P:(t + 1) * P], rt[:, k, :],
                                                    start=(k == 0), stop=(k == KC - 1))
                    last.then_inc(pe_lg, 1)

                def ranks(i, prep):
                    if prep:
                        pe.wait_ge(dve_xtl, KC * (i + 1) + 3)
                    else:
                        pe.wait_ge(act_yrow, TT * NBLK)
                    pe.wait_ge(dve_mask, i + 1)
                    for t in range(TT + 1):
                        for s in range(min(t + 1, TT)):
                            last = nc.tensor.matmul(misc[0][:, t * E:(t + 1) * E], before[:] if s == t else ones[:], mask[:, s, :],
                                                    start=(s == 0), stop=(s == min(t, TT - 1)))
                    last.then_inc(pe_rank, 1)

                def gate(i, c):
                    if c == 0:
                        pe.wait_ge(dve_yl, KC * (i + 1))
                    if some(NCH * i + c):
                        pe.wait_ge(act_sg, NCH * i + c)
                    products(bg[:], lambda a, k: sgw[a][:, k, c * P:(c + 1) * P], lambda b, k: yp[b][:, k, :],
                             range(KC)).then_inc(pe_g, 1)

                def up(i, c):
                    if some(NCH * i + c):
                        pe.wait_ge(dve_h, NCH * i + c)
                    products(bu[:], lambda a, k: suw[a][:, k, c * P:(c + 1) * P], lambda b, k: yp[b][:, k, :],
                             range(KC)).then_inc(pe_u, 1)

                def down(i, c):
                    pe.wait_ge(dve_hl, NCH * i + c + 1)
                    if c == 0:
                        if some(TT * i):
                            pe.wait_ge(dve_o, TT * i)
                    for t in range(TT):
                        last = products(bo[t][:], lambda a, k: hp[a][:, c % 2, t * P:(t + 1) * P], lambda b, k: sdw[b][:, k, :],
                                        [c], start=(c == 0), stop=(c == NCH - 1))
                    last.then_inc(pe_d, 1)

                def body(i, prep):
                    for c in range(NCH):
                        gate(i, c)
                        up(i, c)
                        if c:
                            down(i, c - 1)
                        if prep and c in (0, 1):
                            turn_x(i + 1, 2 * c, False)
                            turn_x(i + 1, 2 * c + 1, False)
                        if c == 2:
                            ranks(i, prep)
                        if prep and c in (3, 4):
                            make_y(i + 1, 2 * (c - 3), False)
                            make_y(i + 1, 2 * (c - 3) + 1, False)
                        if prep and c in (5, 6):
                            turn_y(i + 1, 2 * (c - 5))
                            turn_y(i + 1, 2 * (c - 5) + 1)
                        if prep and c == 7:
                            route(i + 1)
                    down(i, NCH - 1)

                for k in range(KC):
                    turn_x(0, k, True)
                for m in range(KC):
                    make_y(0, m, True)
                for t in range(TT):
                    turn_y(0, t)
                route(0)
                body(0, True)
                with pe.Fori(1, NBLK - 1) as i:
                    body(i, True)
                body(NBLK - 1, False)

            @blk.scalar
            def _(act):
                def x_high(q, k):
                    act.wait_ge(pe_tx, KC * q + k + 1)
                    if k == 0:
                        act.wait_ge(dve_cur, q + 1)
                        if some(KC * q):
                            act.wait_ge(pe_y, KC * q)
                    nc.scalar.activation(xt[0][:, k, :], misc[k % 2][:], ACT.Copy, scale=cur[:, k:k + 1]).then_inc(act_xth, 1)

                def y_scale(q, m):
                    act.wait_ge(pe_y, KC * q + m + 1)
                    if m == 0:
                        if some(q):
                            act.wait_ge(pe_lg, q)
                        if some(KC * q):
                            act.wait_ge(dve_yl, KC * q)
                    nc.scalar.activation(yt[:, m, :], misc[(m + 1) % 2][:], ACT.Identity, scale=cur[:, KC + m:KC + m + 1],
                                         bias=bias_c[:, m:m + 1]).then_inc(act_y, 1)

                def y_row(q, t):
                    act.wait_ge(pe_ty, TT * q + t + 1)
                    if some(16 * (TT // 2 * q + t // 2)):
                        act.wait_ge(y_st[t % 2], 16 * (TT // 2 * q + t // 2))
                    nc.scalar.copy(yrow[:, t % 2, :], misc[(t + 1) % 2][:]).then_inc(act_yrow, 1)

                def y_high(q):
                    act.wait_ge(dve_y, KC * (q + 1))
                    if some(NCH * q):
                        act.wait_ge(pe_u, NCH * q)
                    for k in range(KC):
                        nc.scalar.copy(yp[0][:, k, :], yt[:, k, :]).then_inc(act_yh, 1)

                def scores(q):
                    act.wait_ge(pe_lg, q + 1)
                    if some(q):
                        act.wait_ge(dve_sc, q)
                    nc.scalar.activation(sc[:].rearrange("p t e -> p (t e)"), misc[1][:, 0:TT * E], ACT.Sigmoid).then_inc(act_sc, 1)

                def gate(i, c):
                    act.wait_ge(pe_g, NCH * i + c + 1)
                    if some(NCH * i + c):
                        act.wait_ge(dve_h, NCH * i + c)
                    nc.scalar.activation(sg[:], bg[:], ACT.Silu).then_inc(act_sg, 1)

                def h_high(i, c):
                    act.wait_ge(dve_h, NCH * i + c + 1)
                    if some(NCH * i + max(c - 1, 0)):
                        act.wait_ge(pe_d, NCH * i + max(c - 1, 0))
                    nc.scalar.copy(hp[0][:, c % 2, :], hf[:, c % 2, :]).then_inc(act_hh, 1)

                def body(i, prep):
                    for c in range(NCH):
                        gate(i, c)
                        h_high(i, c)
                        if prep and c in (0, 1):
                            x_high(i + 1, 2 * c)
                            x_high(i + 1, 2 * c + 1)
                        if prep and c in (3, 4):
                            y_scale(i + 1, 2 * (c - 3))
                            y_scale(i + 1, 2 * (c - 3) + 1)
                        if prep and c in (5, 6):
                            y_row(i + 1, 2 * (c - 5))
                            y_row(i + 1, 2 * (c - 5) + 1)
                    if prep:
                        y_high(i + 1)
                        scores(i + 1)

                for k in range(KC):
                    x_high(0, k)
                for m in range(KC):
                    y_scale(0, m)
                for t in range(TT):
                    y_row(0, t)
                y_high(0)
                scores(0)
                body(0, True)
                with act.Fori(1, NBLK - 1) as i:
                    body(i, True)
                body(NBLK - 1, False)

            STEPS = 20 + 3 * TT + 5 * TT

            @blk.vector
            def _(dve):
                def take_cur(q):
                    if some(KC * q):
                        dve.wait_ge(act_y, KC * q)
                    nc.vector.tensor_copy(cur[:], styles[:, bass.ds(q, 1), :].rearrange("p a k -> p (a k)")).then_inc(dve_cur, 1)

                def x_low(q, k):
                    dve.wait_ge(act_xth, KC * q + k + 1)
                    nc.vector.scalar_tensor_tensor(out=xt[1][:, k, :], in0=misc[k % 2][:], scalar=cur[:, k:k + 1],
                                                   in1=xt[0][:, k, :].bitcast(F32), op0=ALU.mult,
                                                   op1=ALU.subtract).then_inc(dve_xtl, 1)

                def y_clip(q, m):
                    dve.wait_ge(act_y, KC * q + m + 1)
                    nc.vector.tensor_scalar(yt[:, m, :], yt[:, m, :], CLAMP, -CLAMP, ALU.min, ALU.max).then_inc(dve_y, 1)

                def y_low(q):
                    for k in range(KC):
                        dve.wait_ge(act_yh, KC * q + k + 1)
                        sub_exact(nc, yp[1][:, k, :], yt[:, k, :], yp[0][:, k, :]).then_inc(dve_yl, 1)

                def hidden(i, c):
                    dve.wait_ge(act_sg, NCH * i + c + 1)
                    dve.wait_ge(pe_u, NCH * i + c + 1)
                    nc.vector.tensor_tensor(hf[:, c % 2, :], bu[:], sg[:], ALU.mult).then_inc(dve_h, 1)
                    dve.wait_ge(act_hh, NCH * i + c + 1)
                    sub_exact(nc, hp[1][:, c % 2, :], hf[:, c % 2, :], hp[0][:, c % 2, :]).then_inc(dve_hl, 1)

                def result(i):
                    dve.wait_ge(xres_ld, 16 * (i + 1))
                    dve.wait_ge(pe_d, NCH * (i + 1))
                    for t in range(TT):
                        nc.vector.tensor_tensor(xres[:, t, :], bo[t][:], xres[:, t, :], ALU.add).then_inc(dve_o, 1)

                flat = "p t e -> p (t e)"

                def by_group(ap):
                    return ap.rearrange("p t (g e) -> p t g e", g=GROUPS)

                def routing(i):
                    n = [0]

                    def link(ins):
                        n[0] += 1
                        ins.then_inc(steps, 1)
                        dve.wait_ge(steps, STEPS * i + n[0])

                    def grouped(ap):
                        return ap.rearrange("p t g -> p (t g)")

                    dve.wait_ge(act_sc, i + 1)
                    link(nc.vector.tensor_tensor(sbi[:], sc[:], eb[:].unsqueeze(1).to_broadcast([P, TT, E]), ALU.add))
                    link(nc.vector.tensor_reduce(g1[:], by_group(sbi[:]), AX_X, ALU.max))
                    link(nc.vector.tensor_tensor(by_group(t1[:]), by_group(sbi[:]),
                                                 g1[:].unsqueeze(3).to_broadcast([P, TT, GROUPS, EPG]), ALU.is_equal))
                    nc.vector.tensor_reduce(g2[:], by_group(t1[:]), AX_X, ALU.add)
                    link(nc.vector.scalar_tensor_tensor(out=t2[:], in0=t1[:], scalar=NEG, in1=sbi[:], op0=ALU.mult, op1=ALU.add))
                    nc.vector.tensor_reduce(g3[:], by_group(t2[:]), AX_X, ALU.max)
                    link(nc.vector.tensor_scalar(g2[:], g2[:], 1.5, NEG, ALU.is_lt, ALU.mult))
                    link(nc.vector.tensor_tensor(g2[:], g2[:], g1[:], ALU.add))
                    link(nc.vector.tensor_tensor(g2[:], g2[:], g3[:], ALU.max))
                    link(nc.vector.tensor_tensor(g1[:], g1[:], g2[:], ALU.add))
                    yield
                    mine = g1[:].unsqueeze(3).to_broadcast([P, TT, GROUPS, GROUPS])
                    theirs = g1[:].unsqueeze(2).to_broadcast([P, TT, GROUPS, GROUPS])
                    nc.vector.tensor_tensor(by_group(t1[:]), theirs, mine, ALU.is_equal)
                    link(nc.vector.tensor_tensor(by_group(t2[:]), theirs, mine, ALU.is_gt))
                    link(nc.vector.tensor_tensor(by_group(t1[:]), by_group(t1[:]),
                                                 lower[:].unsqueeze(1).to_broadcast([P, TT, GROUPS, GROUPS]), ALU.mult))
                    link(nc.vector.tensor_tensor(t1[:], t1[:], t2[:], ALU.add))
                    link(nc.vector.tensor_reduce(g2[:], by_group(t1[:]), AX_X, ALU.add))
                    link(nc.vector.tensor_scalar(g2[:], g2[:], TOPG - 0.5, NEG, ALU.is_gt, ALU.mult))
                    link(nc.vector.tensor_tensor(by_group(t1[:]), by_group(sbi[:]),
                                                 g2[:].unsqueeze(3).to_broadcast([P, TT, GROUPS, EPG]), ALU.add))
                    yield
                    for t in range(TT):
                        dve.nop(nofuse=True)
                        link(nc.vector.max(v8[:, t, :], t1[:, t, :]))
                        dve.nop(nofuse=True)
                        link(nc.vector.max_index(i8[:, t, :], v8[:, t, :], t1[:, t, :]))
                        dve.nop(nofuse=True)
                        link(nc.vector.match_replace(t2[:, t, :], v8[:, t, :], t1[:, t, :], TAKEN))
                    nc.vector.tensor_tensor(mask[:], t1[:], t2[:], ALU.not_equal).then_inc(dve_mask, 1)
                    dve.wait_ge(dve_mask, i + 1)
                    yield
                    link(nc.vector.tensor_tensor(wn[:], mask[:], sc[:], ALU.mult))
                    link(nc.vector.tensor_reduce(den[:], wn[:], AX_X, ALU.add))
                    nc.vector.tensor_copy(i8f[:], i8[:])
                    link(nc.vector.tensor_scalar(den[:], den[:], 1e-20, None, ALU.add))
                    nc.vector.reciprocal(rden[:], den[:]).then_inc(dve_sc, 1)
                    dve.wait_ge(pe_rank, i + 1)
                    ranked = misc[0][:, 0:TT * E].rearrange("p (t e) -> p t e", t=TT)
                    link(nc.vector.tensor_tensor(sl[:], ranked, base[:].unsqueeze(1).to_broadcast([P, TT, E]), ALU.add))
                    nc.vector.tensor_tensor(base[:], misc[0][:, TT * E:(TT + 1) * E], base[:], ALU.add).then_inc(dve_rank, 1)
                    if some(16 * TOPK * TT * i):
                        dve.wait_ge(scattered, 16 * TOPK * TT * i)
                    link(nc.vector.tensor_copy(ent[:, :, :, 0], tok[:].unsqueeze(2).to_broadcast([P, TT, TOPK])))
                    link(nc.vector.tensor_scalar(tok[:], tok[:], float(TB), None, ALU.add))
                    yield
                    for t in range(TT):
                        link(nc.vector.tensor_tensor(oh[:], iota_e[:].unsqueeze(1).to_broadcast([P, TOPK, E]),
                                                     i8f[:, t, :].unsqueeze(2).to_broadcast([P, TOPK, E]), ALU.is_equal))
                        link(nc.vector.tensor_tensor(oh2[:], oh[:], sl[:, t, :].unsqueeze(1).to_broadcast([P, TOPK, E]), ALU.mult))
                        link(nc.vector.tensor_reduce(pf[:, t, :], oh2[:], AX_X, ALU.add))
                        nc.vector.tensor_copy(pos[:, t, :], pf[:, t, :])
                        link(nc.vector.tensor_tensor(oh2[:], oh[:], wn[:, t, :].unsqueeze(1).to_broadcast([P, TOPK, E]), ALU.mult))
                        link(nc.vector.tensor_reduce(v8[:, t, :], oh2[:], AX_X, ALU.add))
                        nc.vector.tensor_scalar(ent[:, t, :, 1].bitcast(F32), v8[:, t, :], rden[:, t:t + 1], None,
                                                ALU.mult).then_inc(dve_ent, 1)
                        yield
                    assert n[0] == STEPS, n[0]

                pieces_of = {0: 2, 1: 1, 3: 1, 4: 1, 5: 2, 6: 2}

                def body(i, prep):
                    pieces = routing(i)
                    for c in range(NCH):
                        hidden(i, c)
                        if prep and c == 0:
                            take_cur(i + 1)
                        if prep and c in (0, 1):
                            x_low(i + 1, 2 * c)
                            x_low(i + 1, 2 * c + 1)
                        if c == 3:
                            next(pieces)
                        if prep and c in (3, 4):
                            y_clip(i + 1, 2 * (c - 3))
                            y_clip(i + 1, 2 * (c - 3) + 1)
                        if prep and c == NCH - 1:
                            y_low(i + 1)
                        if c != 3:
                            for _ in range(pieces_of.get(c, 0)):
                                next(pieces, None)
                    result(i)

                take_cur(0)
                for k in range(KC):
                    x_low(0, k)
                for m in range(KC):
                    y_clip(0, m)
                y_low(0)
                body(0, True)
                with dve.Fori(1, NBLK - 1) as i:
                    body(i, True)
                body(NBLK - 1, False)
        dense.close()

        RING = 3

        with ExitStack() as tmp:
            sb = sb_in(tmp)
            cnt = sb("cnt", [P, E])
            cnt_i = sb("cnt_i", [P, E], I32)
            tiles = sb("tiles", [P, E])
            used = sb("used", [P, E])
            one_e = sb("one_e", [P, E])
            end = sb("end", [P, E])
            j_i = sb("j_i", [P, TQ], I32)
            jf = sb("jf", [P, TQ])
            past = sb("past", [P, TQ, E])
            prod = sb("prod", [P, TQ, E])
            eid, start, order, tmp_q = (sb(n, [P, TQ]) for n in ("eid", "start", "order", "tmp_q"))
            order_i = sb("order_i", [P, TQ], I32)
            tab = sb("tab", [P, TQ, FLD], I32)
            j_made, tab_ok, tab_st = sem("j_made"), sem("tab_ok"), sem("tab_st")
            chain = sem("table_chain")
            THIRD, THIRD_BITS = 43691, 17
            assert all(n * THIRD >> THIRD_BITS == n // RING for n in range(E + 1)) and E * THIRD < 1 << 24
            blk = tmp.enter_context(nc.Block())

            @blk.gpsimd
            def _(pool):
                nc.gpsimd.iota(j_i[:], pattern=[[P, TQ]], base=0, channel_multiplier=1).then_inc(j_made, 1)

            @blk.vector
            def _(dve):
                n_link = [0]

                def link(ins):
                    n_link[0] += 1
                    ins.then_inc(chain, 1)
                    dve.wait_ge(chain, n_link[0])

                def over_tiles(ap):
                    return ap.unsqueeze(1).to_broadcast([P, TQ, E])

                link(nc.vector.tensor_tensor(cnt[:], base[:], base0[:], ALU.subtract))
                link(nc.vector.tensor_scalar(used[:], cnt[:], 0.5, None, ALU.is_gt))
                link(nc.vector.tensor_scalar(cnt_i[:], cnt[:], float(P - 1), None, ALU.add))
                link(nc.vector.tensor_scalar(cnt_i[:], cnt_i[:], LOG_P, None, ALU.arith_shift_right))
                link(nc.vector.tensor_copy(tiles[:], cnt_i[:]))
                link(nc.vector.memset(one_e[:], 1.0))
                link(nc.vector.tensor_tensor_scan(end[:], one_e[:], tiles[:], 0.0, ALU.mult, ALU.add))
                dve.wait_ge(j_made, 1)
                link(nc.vector.tensor_copy(jf[:], j_i[:]))
                link(nc.vector.tensor_tensor(past[:], over_tiles(end[:]), jf[:].unsqueeze(2).to_broadcast([P, TQ, E]), ALU.is_le))
                link(nc.vector.tensor_reduce(eid[:], past[:], AX_X, ALU.add))
                link(nc.vector.tensor_tensor(prod[:], past[:], over_tiles(tiles[:]), ALU.mult))
                link(nc.vector.tensor_reduce(start[:], prod[:], AX_X, ALU.add))
                link(nc.vector.tensor_tensor(prod[:], past[:], over_tiles(used[:]), ALU.mult))
                link(nc.vector.tensor_reduce(order[:], prod[:], AX_X, ALU.add))
                link(nc.vector.tensor_tensor(tmp_q[:], jf[:], start[:], ALU.subtract))
                link(nc.vector.tensor_scalar(tmp_q[:], tmp_q[:], float(P), None, ALU.mult))
                link(nc.vector.scalar_tensor_tensor(out=tab[:, :, 0], in0=eid[:], scalar=float(REG), in1=tmp_q[:],
                                                    op0=ALU.mult, op1=ALU.add))
                link(nc.vector.tensor_copy(tab[:, :, 1], order[:]))
                link(nc.vector.tensor_scalar(tab[:, :, 2], eid[:], float(E - 1), None, ALU.min))
                link(nc.vector.tensor_copy(tab[:, :, 3], start[:]))
                link(nc.vector.tensor_tensor(tab[:, :, 4], jf[:], start[:], ALU.is_equal))
                link(nc.vector.tensor_scalar(order_i[:], order[:], float(THIRD), None, ALU.mult))
                link(nc.vector.tensor_scalar(order_i[:], order_i[:], THIRD_BITS, None, ALU.arith_shift_right))
                link(nc.vector.tensor_copy(tmp_q[:], order_i[:]))
                link(nc.vector.scalar_tensor_tensor(out=tab[:, :, 5], in0=tmp_q[:], scalar=-float(RING), in1=order[:],
                                                    op0=ALU.mult, op1=ALU.add))
                link(nc.vector.tensor_copy(tab[:, :, 6], end[:, E - 1:E].to_broadcast([P, TQ])))
                link(nc.vector.tensor_scalar(jf[:], jf[:], -1.0, None, ALU.add))
                link(nc.vector.tensor_tensor(past[:], over_tiles(end[:]), jf[:].unsqueeze(2).to_broadcast([P, TQ, E]), ALU.is_le))
                link(nc.vector.tensor_tensor(prod[:], past[:], over_tiles(tiles[:]), ALU.mult))
                link(nc.vector.tensor_reduce(start[:], prod[:], AX_X, ALU.add))
                nc.vector.tensor_copy(tab[:, :, 7], start[:]).then_inc(tab_ok, 1)

            @blk.sync
            def _(sp):
                sp.wait_ge(tab_ok, 1)
                sp.dma_start(table.rearrange("(q p) f -> p q f", p=P), tab[:]).then_inc(tab_st, 16)
                sp.wait_ge(tab_st, 16)

        with ExitStack() as tmp:
            sb = sb_in(tmp)
            trow = sb("trow", [1, TQ * P * FLD], I32)
            raw = [sb("raw_gu", [P, KC, 2 * H]), sb("raw_d", [P, KH, C])]
            wgu = [sb("w_gu_h", [P, RING, KC, 2 * H], F32R), sb("w_gu_l", [P, RING, KC, 2 * H], F32R)]
            wdn = [sb("w_dn_h", [P, RING, KH, C], F32R), sb("w_dn_l", [P, RING, KH, C], F32R)]
            lg = [sb(f"list_g{n}", [P, 2], I32) for n in range(UN)]
            ls = [sb(f"list_s{n}", [P, 2], I32) for n in range(UN)]
            xg = [sb(f"x_rows{n}", [P, C]) for n in range(UN)]
            xp = [sb("x_h", [P, 2, KC, P], F32R), sb("x_l", [P, 2, KC, P], F32R)]
            sg = sb("e_sg", [P, 2, H])
            hf = sb("e_hf", [P, 2, H])
            hp = [sb("e_h_h", [P, 2, KH, P], F32R), sb("e_h_l", [P, 2, KH, P], F32R)]
            og = [sb(f"o_rows{n}", [P, C]) for n in range(UN)]

            b_gu, b_x, b_h, b_o = bank[0:2], bank[2:4], bank[4:6], bank[6:8]

            tab_ld, raw_ld = sem("tab_ld"), sem("raw_ld")
            lg_ld = [sem(f"lg_ld{n}") for n in range(UN)]
            ls_ld = [sem(f"ls_ld{n}") for n in range(UN)]
            x_ld = [sem(f"x_rows_ld{n}") for n in range(UN)]
            added = sem("added")
            split = sem("split")
            pe_x, act_x, dve_x = sem("pe_x"), sem("act_x"), sem("dve_x")
            pe_gu, act_gu, dve_gu = sem("pe_gu"), sem("act_gu"), sem("dve_gu")
            pe_ht, act_ht, dve_ht = sem("pe_ht"), sem("act_ht"), sem("dve_ht")
            pe_do = sem("pe_do")
            act_do = sem("act_do")
            wsteps = sem("split_steps")
            fin = sem("fin")
            blk = tmp.enter_context(nc.Block())

            NTURN = MAXT // UN
            assert MAXT % UN == 0 and NTURN > 2
            LAG_S = 5

            def field(eng, j, f, top_val):
                return eng.value_load(trow[0:1, bass.ds(j * FLD + f, 1)], min_val=0, max_val=top_val)


            @blk.sync
            def _(sp):
                sp.dma_start(trow[:], table.rearrange("(a j) f -> a (j f)", a=1)).then_inc(tab_ld, 16)
                sp.wait_ge(tab_ld, 16)

                def load_list(dst, s, j):
                    off = field(sp, j, 0, LROWS - P)
                    sp.dma_start(dst[:], slots[bass.ds(off, P), :]).then_inc(s, 16)

                def weights(j):
                    with sp.If(field(sp, j, 4, 1) > 0):
                        order = field(sp, j, 1, E)
                        e = field(sp, j, 2, E - 1)
                        sp.wait_ge(split, order + 1)
                        for n, w in enumerate((gate_w, up_w)):
                            sp.dma_start(raw[0][:, :, n * H:(n + 1) * H],
                                         w[bass.ds(e, 1)].rearrange("e (k p) h -> p (e k) h", p=P)).then_inc(raw_ld, 16)
                        sp.dma_start(raw[1][:], down_w[bass.ds(e, 1)].rearrange("e (k p) h -> p (e k) h", p=P)).then_inc(raw_ld, 16)

                def step(g, u):
                    n = g * UN + u
                    known = isinstance(n, int)
                    if not known or n >= UN:
                        sp.wait_ge(x_ld[u], 16 * g)
                    load_list(lg[u], lg_ld[u], n)
                    if not known or n >= 1:
                        weights(n - 1)
                    if not known or n >= LAG_S:
                        m = n - LAG_S
                        if not known or m >= UN:
                            sp.wait_ge(added, 16 * (m - UN + 1))
                        load_list(ls[(u - LAG_S) % UN], ls_ld[(u - LAG_S) % UN], m)

                for n in range(3 * UN):
                    step(n // UN, n % UN)
                with sp.Fori(3, NTURN + 1) as g:
                    for u in range(UN):
                        step(g, u)
                for m in range(MAXT + UN - LAG_S, MAXT):
                    sp.wait_ge(added, 16 * (m - UN + 1))
                    load_list(ls[m % UN], ls_ld[m % UN], m)
                sp.wait_ge(added, 16 * MAXT)
                sp.dma_start(of, acc[0:N, :]).then_inc(fin, 16)
                sp.wait_ge(fin, 16)

            @blk.gpsimd
            def _(pool):
                def gather(g, u):
                    pool.wait_ge(lg_ld[u], 16 * (g + 1))
                    pool.nop(nofuse=True)
                    nc.gpsimd.indirect_dma_start(xg[u][:], None, y_rows,
                                                 bass.IndirectOffsetOnAxis(ap=lg[u][:, 0:1].bitcast(U32), axis=0)).then_inc(x_ld[u], 16)

                def scatter(m, u, gm):
                    pool.wait_ge(act_do, m + 1)
                    pool.wait_ge(ls_ld[u], 16 * (gm + 1))
                    if not isinstance(m, int) or m >= 1:
                        pool.wait_ge(added, 16 * m)
                    pool.nop(nofuse=True)
                    nc.gpsimd.indirect_dma_start(acc, bass.IndirectOffsetOnAxis(ap=ls[u][:, 0:1].bitcast(U32), axis=0),
                                                 og[u][:], None, compute_op=ALU.add).then_inc(added, 16)

                def step(g, u):
                    j = g * UN + u
                    pool.wait_ge(pe_x, j + 1)
                    gather(g + 1, u)
                    if not isinstance(j, int) or j >= 3:
                        scatter(j - 3, (u - 3) % UN, g - 1 if u < 3 else g)

                for u in range(UN):
                    gather(0, u)
                for u in range(UN):
                    step(0, u)
                for u in range(UN):
                    step(1, u)
                with pool.Fori(2, NTURN) as g:
                    for u in range(UN):
                        step(g, u)
                for m in range(MAXT - 3, MAXT):
                    scatter(m, m % UN, m // UN)
                for u in range(UN):
                    pool.wait_ge(x_ld[u], 16 * (NTURN + 1))
                pool.wait_ge(added, 16 * MAXT)

            @blk.tensor
            def _(pe):
                pe.wait_ge(tab_ld, 16)
                pe.sem_inc(pe_do, 1)

                def turn_x(j, u, g):
                    if not isinstance(j, int) or j >= 2:
                        pe.wait_ge(dve_x, j - 1)
                    pe.wait_ge(x_ld[u], 16 * (g + 1))
                    for k in range(KC):
                        last = nc.tensor.transpose(b_x[u % 2][:, k * P:(k + 1) * P], xg[u][:, k * P:(k + 1) * P], ident[:])
                    last.then_inc(pe_x, 1)

                def gate_up(j, u, place, chunks):
                    for k in chunks:
                        if k == 0:
                            if not isinstance(j, int) or j >= 2:
                                pe.wait_ge(dve_gu, j - 1)
                            pe.wait_ge(dve_x, j + 1)
                        for a, b in ((0, 0), (0, 1), (1, 0)):
                            last = nc.tensor.matmul(b_gu[u % 2][:], xp[a][:, u % 2, k, :],
                                                    wgu[b][:, bass.ds(place, 1), k, :].rearrange("p a n -> p (a n)"),
                                                    start=(k == 0 and a == b == 0), stop=(k == KC - 1 and a == 1))
                    if KC - 1 in chunks:
                        last.then_inc(pe_gu, 1)

                def turn_h(j, u):
                    if not isinstance(j, int) or j >= 2:
                        pe.wait_ge(dve_ht, j - 1)
                    pe.wait_ge(dve_gu, j + 1)
                    for k in range(KH):
                        last = nc.tensor.transpose(b_h[u % 2][:, k * P:(k + 1) * P], hf[:, u % 2, k * P:(k + 1) * P], ident[:])
                    last.then_inc(pe_ht, 1)

                def down(j, u, place):
                    if not isinstance(j, int) or j >= 2:
                        pe.wait_ge(act_do, j - 1)
                    pe.wait_ge(dve_ht, j + 1)
                    for k in range(KH):
                        for a, b in ((0, 0), (0, 1), (1, 0)):
                            last = nc.tensor.matmul(b_o[u % 2][:], hp[a][:, u % 2, k, :],
                                                    wdn[b][:, bass.ds(place, 1), k, :].rearrange("p a n -> p (a n)"),
                                                    start=(k == 0 and a == b == 0), stop=(k == KH - 1 and a == 1))
                    last.then_inc(pe_do, 1)

                def step(g, u):
                    j = g * UN + u
                    before_it = not isinstance(j, int) or j >= 1
                    turn_x(j + 1, (u + 1) % UN, g + 1 if u == UN - 1 else g)
                    order, place = field(pe, j, 1, E), field(pe, j, 5, RING - 1)
                    pe.wait_ge(split, order + 2)
                    gate_up(j, u, place, range(0, KC // 2))
                    if before_it:
                        turn_h(j - 1, (u - 1) % UN)
                    gate_up(j, u, place, range(KC // 2, KC))
                    if before_it:
                        down(j - 1, (u - 1) % UN, field(pe, j - 1, 5, RING - 1))

                turn_x(0, 0, 0)
                for u in range(UN):
                    step(0, u)
                for u in range(UN):
                    step(1, u)
                with pe.Fori(2, NTURN) as g:
                    for u in range(UN):
                        step(g, u)
                turn_h(MAXT - 1, UN - 1)
                down(MAXT - 1, UN - 1, field(pe, MAXT - 1, 5, RING - 1))

            @blk.scalar
            def _(act):
                def x_high(j, u):
                    act.wait_ge(pe_x, j + 1)
                    if not isinstance(j, int) or j >= 2:
                        act.wait_ge(pe_gu, j - 1)
                    nc.scalar.copy(xp[0][:, u % 2, :, :].rearrange("p k t -> p (k t)"), b_x[u % 2][:]).then_inc(act_x, 1)

                def silu(j, u):
                    act.wait_ge(pe_gu, j + 1)
                    if not isinstance(j, int) or j >= 2:
                        act.wait_ge(dve_gu, j - 1)
                    nc.scalar.activation(sg[:, u % 2, :], b_gu[u % 2][:, 0:H], ACT.Silu).then_inc(act_gu, 1)

                def h_high(j, u):
                    act.wait_ge(pe_ht, j + 1)
                    if not isinstance(j, int) or j >= 2:
                        act.wait_ge(pe_do, j)
                    nc.scalar.copy(hp[0][:, u % 2, :, :].rearrange("p k t -> p (k t)"), b_h[u % 2][:, 0:H]).then_inc(act_ht, 1)

                def weigh(j, u, g):
                    act.wait_ge(pe_do, j + 2)
                    act.wait_ge(ls_ld[u], 16 * (g + 1))
                    if not isinstance(j, int) or j >= UN:
                        act.wait_ge(added, 16 * (j - UN + 1))
                    nc.scalar.activation(og[u][:], b_o[u % 2][:], ACT.Copy, scale=ls[u][:, 1:2].bitcast(F32)).then_inc(act_do, 1)

                def step(g, u):
                    j = g * UN + u
                    known = isinstance(j, int)
                    x_high(j + 1, (u + 1) % UN)
                    if not known or j >= 2:
                        weigh(j - 2, (u - 2) % UN, g - 1 if u < 2 else g)
                    if not known or j >= 1:
                        h_high(j - 1, (u - 1) % UN)
                    silu(j, u)

                x_high(0, 0)
                for u in range(UN):
                    step(0, u)
                for u in range(UN):
                    step(1, u)
                with act.Fori(2, NTURN) as g:
                    for u in range(UN):
                        step(g, u)
                weigh(MAXT - 2, UN - 2, NTURN - 1)
                h_high(MAXT - 1, UN - 1)
                weigh(MAXT - 1, UN - 1, NTURN - 1)

            @blk.vector
            def _(dve):
                dve.wait_ge(tab_ld, 16)
                dve.sem_inc(split, 1)

                def x_low(j, u):
                    dve.wait_ge(act_x, j + 1)
                    sub_exact(nc, xp[1][:, u % 2, :, :].rearrange("p k t -> p (k t)"), b_x[u % 2][:],
                              xp[0][:, u % 2, :, :].rearrange("p k t -> p (k t)")).then_inc(dve_x, 1)

                def hidden(j, u):
                    dve.wait_ge(act_gu, j + 1)
                    if not isinstance(j, int) or j >= 2:
                        dve.wait_ge(pe_ht, j - 1)
                    nc.vector.tensor_tensor(hf[:, u % 2, :], b_gu[u % 2][:, H:2 * H], sg[:, u % 2, :], ALU.mult).then_inc(dve_gu, 1)

                def h_low(j, u):
                    dve.wait_ge(act_ht, j + 1)
                    sub_exact(nc, hp[1][:, u % 2, :, :].rearrange("p k t -> p (k t)"), b_h[u % 2][:, 0:H],
                              hp[0][:, u % 2, :, :].rearrange("p k t -> p (k t)")).then_inc(dve_ht, 1)

                def split_weights(j):
                    first = isinstance(j, int) and j == 0
                    with dve.If(field(dve, j, 4, 1) > 0):
                        order = field(dve, j, 1, E)
                        place = field(dve, j, 5, RING - 1)
                        if not first:
                            dve.wait_ge(pe_do, field(dve, field(dve, j - 1, 3, MAXT), 7, MAXT) + 1)
                        dve.wait_ge(raw_ld, order * 48 + 48)
                        nc.vector.tensor_copy(wgu[0][:, bass.ds(place, 1), :, :].rearrange("p a k n -> p (a k) n"), raw[0][:]).then_inc(wsteps, 1)
                        nc.vector.tensor_copy(wdn[0][:, bass.ds(place, 1), :, :].rearrange("p a k n -> p (a k) n"), raw[1][:]).then_inc(wsteps, 1)
                        dve.wait_ge(wsteps, order * 3 + 1)
                        sub_exact(nc, wgu[1][:, bass.ds(place, 1), :, :].rearrange("p a k n -> p (a k) n"), raw[0][:],
                                  wgu[0][:, bass.ds(place, 1), :, :].rearrange("p a k n -> p (a k) n")).then_inc(wsteps, 1)
                        dve.wait_ge(wsteps, order * 3 + 3)
                        sub_exact(nc, wdn[1][:, bass.ds(place, 1), :, :].rearrange("p a k n -> p (a k) n"), raw[1][:],
                                  wdn[0][:, bass.ds(place, 1), :, :].rearrange("p a k n -> p (a k) n")).then_inc(split, 1)

                def step(g, u):
                    j = g * UN + u
                    x_low(j + 1, (u + 1) % UN)
                    if not isinstance(j, int) or j >= 1:
                        h_low(j - 1, (u - 1) % UN)
                    hidden(j, u)
                    split_weights(j + 2)

                split_weights(0)
                x_low(0, 0)
                split_weights(1)
                for u in range(UN):
                    step(0, u)
                for u in range(UN):
                    step(1, u)
                with dve.Fori(2, NTURN) as g:
                    for u in range(UN):
                        step(g, u)
                h_low(MAXT - 1, UN - 1)


_INS = ['x', 'cond_512', 'L0_cond_weight', 'L0_cond_bias', 'L0_cond_affine_w', 'L0_cond_affine_b', 'L0_ffn_router_w',
        'L0_ffn_e_bias', 'L0_ffn_gate_w', 'L0_ffn_up_w', 'L0_ffn_down_w', 'L0_ffn_sh_gate_w', 'L0_ffn_sh_up_w',
        'L0_ffn_sh_down_w']
_OUTS = [((8, 1024, 512), 'float32')]


def kernel(**inputs):
    import numpy as _np
    import concourse.bacc as _bacc
    from concourse import mybir as _mybir
    from concourse.bass_utils import run_bass_kernel_spmd as _run

    nc = _bacc.Bacc("TRN2", target_bir_lowering=False, num_devices=1)
    arrays, args = {}, []
    for name in _INS:
        a = _np.ascontiguousarray(inputs[name])
        arrays[f"in_{name}_dram"] = a
        args.append(nc.dram_tensor(f"in_{name}_dram", a.shape, _mybir.dt.from_np(a.dtype), kind="ExternalInput").ap())
    for i, (shape, dtype) in enumerate(_OUTS):
        dt = _mybir.dt.from_np(_np.dtype(dtype))
        args.append(nc.dram_tensor(f"out_{i}_dram", shape, dt, kind="ExternalOutput").ap())
    build(nc, *args)
    r = _run(nc, [arrays], core_ids=[0])
    got = tuple(r.results[0][f"out_{i}_dram"] for i in range(len(_OUTS)))
    return got[0]
```

```python
from contextlib import ExitStack

import concourse.bass as bass
from concourse import mybir

ALU = mybir.AluOpType
ACT = mybir.ActivationFunctionType
AX_X = mybir.AxisListType.X
F32 = mybir.dt.float32
F32R = mybir.dt.float32r
BF16 = mybir.dt.bfloat16
I32 = mybir.dt.int32
U32 = mybir.dt.uint32

P = 128

NEG = -3.0e38
TAKEN = -3.3e38


def some(n):
    return not isinstance(n, int) or n > 0


def sub_exact(nc, out, full, high):
    return nc.vector.tensor_tensor(out, full, high.bitcast(F32), ALU.subtract)


def build(nc, x, cond, cw, cbias, aff_w, aff_b, router_w, e_bias, gate_w, up_w, down_w,
          sh_gate, sh_up, sh_down, out):
    B, L, C = x.shape
    N = B * L
    WD = cond.shape[1]
    E, _, H = gate_w.shape
    HS = sh_gate.shape[1]
    TOPK, GROUPS, TOPG = 8, 8, 4
    EPG = E // GROUPS
    CLAMP = 256.0
    KC = C // P
    KH = H // P
    KW = WD // P
    TB = 512
    TT = TB // P
    NBLK = N // TB
    NCH = HS // P
    LOG_P = P.bit_length() - 1
    MAXT = N * TOPK // P + E
    UN = 4
    TQ = -(-(MAXT + 2 * UN) // P)
    REG = N
    LROWS = -(-(E * REG + TQ * P * P) // (P * P)) * P * P
    FLD = 7

    xf = x.rearrange("b l c -> (b l) c")
    of = out.rearrange("b l c -> (b l) c")
    y_rows = nc.dram_tensor("y_rows", (N + P, C), F32).ap()
    acc = nc.dram_tensor("acc_rows", (N + P, C), F32).ap()
    slots = nc.dram_tensor("slot_list", (LROWS, 2), I32).ap()
    table = nc.dram_tensor("tile_table", (TQ * P, FLD), I32).ap()

    top = ExitStack()

    def sem(name):
        return top.enter_context(nc.semaphore(name))

    with top:
        keep = ExitStack()
        top.enter_context(keep)

        def sb_in(stack):
            return lambda name, shape, dt=F32: stack.enter_context(nc.sbuf_tensor(name, shape, dt))

        bank = [top.enter_context(nc.psum_tensor(f"bank{n}", [P, 512], F32)) for n in range(8)]

        sb = sb_in(keep)
        ident = sb("ident", [P, P])
        base = sb("base", [P, E])
        base0 = sb("base0", [P, E])
        zrow = sb("zrow", [P, C])

        dense = ExitStack()
        sb = sb_in(dense)
        sgw = [sb("sh_gate_h", [P, KC, HS], F32R), sb("sh_gate_l", [P, KC, HS], F32R)]
        suw = [sb("sh_up_h", [P, KC, HS], F32R), sb("sh_up_l", [P, KC, HS], F32R)]
        sdw = [sb("sh_down_h", [P, NCH, C], F32R), sb("sh_down_l", [P, NCH, C], F32R)]
        wt = [sb("w_h", [P, KC, C], F32R), sb("w_l", [P, KC, C], F32R)]
        rt = sb("router_t", [P, KC, E])
        bias_c = sb("bias_c", [P, KC])
        styles = sb("styles", [P, NBLK, 2 * KC])
        eb = sb("e_bias_b", [P, E])
        before = sb("before", [P, P], BF16)
        ones = sb("ones", [P, P], BF16)
        iota_e = sb("iota_e", [P, E])
        lower = sb("lower", [P, GROUPS, GROUPS])
        tok = sb("tok", [P, TT], I32)

        with ExitStack() as tmp:
            sb = sb_in(tmp)
            stage = [sb("stage_g", [P, KC, HS]), sb("stage_u", [P, KC, HS]), sb("stage_d", [P, NCH, C])]
            w_raw = sb("w_raw", [P, KC, C])
            aw_raw = sb("aw_raw", [P, KC, WD])
            rw_raw = sb("rw_raw", [E, C])
            cond_raw = sb("cond_raw", [B, WD])
            ab = sb("ab", [P, KC])
            cond_t = sb("cond_t", [P, KW, B])
            aw_t = sb("aw_t", [P, KW, C])
            w_sq = sb("w_sq", [P, KC, C])
            st = sb("st", [P, KC, B])
            st_sq = sb("st_sq", [P, KC, B])
            dco = sb("dco", [P, KC, B])
            sq_sum = sb("sq_sum", [P, KC, B])
            root = sb("root", [P, KC, B])
            pad = sb("pad", [P, P, 2], I32)
            iota_i = sb("iota_i", [P, E], I32)
            low_i = sb("low_i", [P, GROUPS, GROUPS], I32)

            ld_small, ld_w, ld_aff, ld_r = sem("ld_small"), sem("ld_w"), sem("ld_aff"), sem("ld_r")
            ld_sh = [sem("ld_sh_gate"), sem("ld_sh_up"), sem("ld_sh_down")]
            made = sem("made")
            zeroed = sem("zeroed")
            filled = sem("filled")
            turned = sem("turned")
            copied = sem("copied")
            squared = sem("squared")
            high = sem("high")
            low = sem("low")
            st_mm, st_ok, sq_mm = sem("st_mm"), sem("st_ok"), sem("sq_mm")
            chain = sem("setup_chain")
            rooted = sem("rooted")
            ROOT_AT = 6
            blk = tmp.enter_context(nc.Block())

            @blk.sync
            def _(sp):
                sp.dma_start(aw_raw[:], aff_w.rearrange("(k p) w -> p k w", p=P)).then_inc(ld_aff, 16)
                sp.dma_start(cond_raw[:], cond).then_inc(ld_aff, 16)
                sp.dma_start(w_raw[:], cw.rearrange("(k p) c -> p k c", p=P)).then_inc(ld_w, 16)
                sp.dma_start(rw_raw[:], router_w).then_inc(ld_r, 16)
                with nc.allow_non_contiguous_dma(reason="small columns"):
                    sp.dma_start(ab[:], aff_b.rearrange("(k p) -> p k", p=P)).then_inc(ld_small, 16)
                    sp.dma_start(bias_c[:], cbias.rearrange("(k p) -> p k", p=P)).then_inc(ld_small, 16)
                sp.dma_start(eb[:], e_bias.partition_broadcast(P)).then_inc(ld_small, 16)
                for n, w in enumerate((sh_gate, sh_up, sh_down)):
                    sp.dma_start(stage[n][:], w.rearrange("(k p) h -> p k h", p=P)).then_inc(ld_sh[n], 16)
                sp.wait_ge(made, 7)
                per = LROWS // P // P
                sp.dma_start(slots.rearrange("(q a r) k -> q a (r k)", q=P, a=per),
                             pad[:].rearrange("p r k -> p (r k)").unsqueeze(1).to_broadcast([P, per, 2 * P])
                             ).then_inc(filled, 16)
                sp.wait_ge(zeroed, 1)
                sp.dma_start(y_rows[N:N + P, :], zrow[:]).then_inc(filled, 16)
                sp.dma_start(acc[N:N + P, :], zrow[:]).then_inc(filled, 16)
                sp.wait_ge(filled, 48)

            @blk.gpsimd
            def _(pool):
                nc.gpsimd.memset(ident[:], 0.0).then_inc(made, 1)
                pool.wait_ge(made, 1)
                nc.gpsimd.affine_select(out=ident[:], in_=ident[:], compare_op=ALU.not_equal, fill=1.0,
                                        base=0, pattern=[[-1, P]], channel_multiplier=1).then_inc(made, 1)
                nc.gpsimd.memset(ones[:], 1.0).then_inc(made, 1)
                pool.wait_ge(made, 3)
                nc.gpsimd.affine_select(out=before[:], in_=ones[:], compare_op=ALU.is_gt, fill=0.0,
                                        base=0, pattern=[[1, P]], channel_multiplier=-1).then_inc(made, 1)
                nc.gpsimd.memset(pad[:], 0).then_inc(made, 1)
                nc.gpsimd.iota(iota_i[:], pattern=[[1, E]], base=0, channel_multiplier=0).then_inc(made, 1)
                pool.wait_ge(made, 6)
                nc.gpsimd.iota(pad[:, :, 0:1].rearrange("p r k -> p (r k)"), pattern=[[1, P]], base=N,
                               channel_multiplier=0).then_inc(made, 1)
                nc.gpsimd.iota(low_i[:], pattern=[[1, GROUPS], [-1, GROUPS]], base=0,
                               channel_multiplier=0).then_inc(made, 1)
                nc.gpsimd.iota(tok[:], pattern=[[P, TT]], base=0, channel_multiplier=1).then_inc(made, 1)

            @blk.tensor
            def _(pe):
                pe.wait_ge(made, 2)
                pe.wait_ge(ld_aff, 32)
                for k in range(KW):
                    nc.tensor.transpose(bank[0][:, k * B:(k + 1) * B], cond_raw[:, k * P:(k + 1) * P], ident[0:B, 0:B])
                for k in range(KW):
                    for m in range(KC):
                        last = nc.tensor.transpose(bank[1 + k][:, m * P:(m + 1) * P], aw_raw[:, m, k * P:(k + 1) * P], ident[:])
                last.then_inc(turned, 1)
                pe.wait_ge(ld_r, 16)
                for k in range(KC):
                    last = nc.tensor.transpose(bank[3][:, k * E:(k + 1) * E], rw_raw[:, k * P:(k + 1) * P], ident[0:E, 0:E])
                last.then_inc(turned, 1)
                pe.wait_ge(ld_w, 16)
                for k in range(KC):
                    for m in range(KC):
                        last = nc.tensor.transpose(bank[4 + k][:, m * P:(m + 1) * P], w_raw[:, m, k * P:(k + 1) * P], ident[:])
                    last.then_inc(turned, 1)
                pe.wait_ge(copied, 2)
                for m in range(KC):
                    for k in range(KW):
                        last = nc.tensor.matmul(bank[0][:, 64 + m * B:64 + (m + 1) * B], aw_t[:, k, m * P:(m + 1) * P],
                                                cond_t[:, k, :], start=(k == 0), stop=(k == KW - 1))
                last.then_inc(st_mm, 1)
                pe.wait_ge(st_ok, 1)
                pe.wait_ge(squared, KC)
                for m in range(KC):
                    for k in range(KC):
                        last = nc.tensor.matmul(bank[1][:, m * B:(m + 1) * B], w_sq[:, k, m * P:(m + 1) * P],
                                                st_sq[:, k, :], start=(k == 0), stop=(k == KC - 1))
                last.then_inc(sq_mm, 1)

            @blk.scalar
            def _(act):
                for k in range(KC):
                    act.wait_ge(turned, 3 + k)
                    nc.scalar.copy(wt[0][:, k, :], bank[4 + k][:]).then_inc(high, 1)
                    nc.scalar.activation(w_sq[:, k, :], bank[4 + k][:], ACT.Square).then_inc(squared, 1)
                for n, (w, s) in enumerate(((sgw, stage[0]), (suw, stage[1]), (sdw, stage[2]))):
                    act.wait_ge(ld_sh[n], 16)
                    nc.scalar.copy(w[0][:], s[:]).then_inc(high, 1)
                act.wait_ge(chain, ROOT_AT)
                nc.scalar.activation(root[:], sq_sum[:], ACT.Sqrt).then_inc(rooted, 1)

            @blk.vector
            def _(dve):
                n_link = [0]

                def link(ins):
                    n_link[0] += 1
                    ins.then_inc(chain, 1)
                    dve.wait_ge(chain, n_link[0])

                nc.vector.memset(zrow[:], 0.0).then_inc(zeroed, 1)
                dve.wait_ge(made, 9)
                link(nc.vector.tensor_copy(iota_e[:], iota_i[:]))
                link(nc.vector.tensor_scalar(base[:], iota_e[:], float(REG), None, ALU.mult))
                link(nc.vector.tensor_copy(base0[:], base[:]))
                link(nc.vector.tensor_scalar(lower[:], low_i[:], 0.0, None, ALU.is_gt))
                dve.wait_ge(turned, 1)
                nc.vector.tensor_copy(cond_t[:].rearrange("p k b -> p (k b)"), bank[0][:, 0:KW * B])
                for k in range(KW):
                    last = nc.vector.tensor_copy(aw_t[:, k, :], bank[1 + k][:])
                    if k == KW - 1:
                        last.then_inc(copied, 1)
                dve.wait_ge(turned, 2)
                nc.vector.tensor_copy(rt[:].rearrange("p k e -> p (k e)"), bank[3][:, 0:KC * E]).then_inc(copied, 1)
                dve.wait_ge(st_mm, 1)
                dve.wait_ge(ld_small, 48)
                gain = float(WD) ** -0.5
                for m in range(KC):
                    last = nc.vector.tensor_scalar(st[:, m, :], bank[0][:, 64 + m * B:64 + (m + 1) * B], gain, ab[:, m:m + 1],
                                                   ALU.mult, ALU.add)
                link(last)
                nc.vector.tensor_tensor(st_sq[:], st[:], st[:], ALU.mult).then_inc(st_ok, 1)
                for k in range(KC):
                    dve.wait_ge(squared, k + 1)
                    sub_exact(nc, wt[1][:, k, :], bank[4 + k][:], wt[0][:, k, :])
                dve.wait_ge(sq_mm, 1)
                flat_d = "p k b -> p (k b)"
                link(nc.vector.tensor_scalar(sq_sum[:].rearrange(flat_d), bank[1][:, 0:KC * B], 1e-8, None, ALU.add))
                dve.wait_ge(rooted, 1)
                link(nc.vector.reciprocal(dco[:], root[:]))
                link(nc.vector.tensor_tensor(root[:], dco[:], dco[:], ALU.mult))
                link(nc.vector.tensor_tensor(root[:], root[:], sq_sum[:], ALU.mult))
                link(nc.vector.tensor_scalar(root[:], root[:], -0.5, 1.5, ALU.mult, ALU.add))
                link(nc.vector.tensor_tensor(dco[:], dco[:], root[:], ALU.mult))
                per = NBLK // B
                for h in range(per):
                    v = styles[:].rearrange("p (b h) k -> p h k b", h=per)[:, h]
                    nc.vector.tensor_copy(v[:, 0:KC, :], st[:])
                    link(nc.vector.tensor_copy(v[:, KC:2 * KC, :], dco[:]))
                for n, (w, s) in enumerate(((sgw, stage[0]), (suw, stage[1]), (sdw, stage[2]))):
                    dve.wait_ge(high, KC + 1 + n)
                    link(sub_exact(nc, w[1][:], s[:], w[0][:]))

        with ExitStack() as tmp:
            sb = sb_in(tmp)
            xin = sb("xin", [P, TT, C])
            xres = sb("xres", [P, TT, C])
            xt = [sb("xt_h", [P, KC, TB], F32R), sb("xt_l", [P, KC, TB], F32R)]
            yt = sb("yt", [P, KC, TB])
            yp = [sb("y_h", [P, KC, TB], F32R), sb("y_l", [P, KC, TB], F32R)]
            yrow = sb("yrow", [P, 2, C])
            cur = sb("cur", [P, 2 * KC])
            sg = sb("sg", [P, TB])
            hf = sb("hf", [P, 2, TB])
            hp = [sb("h_h", [P, 2, TB], F32R), sb("h_l", [P, 2, TB], F32R)]
            sc = sb("sc", [P, TT, E])
            sbi = sb("sbi", [P, TT, E])
            t1 = sb("t1", [P, TT, E])
            t2 = sb("t2", [P, TT, E])
            mask = sb("mask", [P, TT, E], BF16)
            wn = sb("wn", [P, TT, E])
            sl = sb("sl", [P, TT, E])
            g1, g2, g3 = (sb(f"g{n}", [P, TT, GROUPS]) for n in range(3))
            v8 = sb("v8", [P, TT, TOPK])
            i8 = sb("i8", [P, TT, TOPK], U32)
            i8f = sb("i8f", [P, TT, TOPK])
            pf = sb("pf", [P, TT, TOPK])
            pos = sb("pos", [P, TT, TOPK], U32)
            ent = sb("ent", [P, TT, TOPK, 2], I32)
            den = sb("den", [P, TT])
            rden = sb("rden", [P, TT])
            oh = sb("oh", [P, TOPK, E])
            oh2 = sb("oh2", [P, TOPK, E])

            bg, bu = bank[0], bank[1]
            bo = bank[2:6]
            misc = bank[6:8]

            x_ld, xres_ld, o_st = sem("x_ld"), sem("xres_ld"), sem("o_st")
            y_st = [sem("y_st0"), sem("y_st1")]
            pe_tx, act_xth, dve_xtl = sem("pe_tx"), sem("act_xth"), sem("dve_xtl")
            pe_y, act_y, dve_y = sem("pe_y"), sem("act_y"), sem("dve_y")
            pe_ty, act_yrow = sem("pe_ty"), sem("act_yrow")
            act_yh, dve_yl = sem("act_yh"), sem("dve_yl")
            pe_lg, act_sc, dve_sc = sem("pe_lg"), sem("act_sc"), sem("dve_sc")
            pe_g, act_sg, pe_u, dve_h = sem("pe_g"), sem("act_sg"), sem("pe_u"), sem("dve_h")
            act_hh, dve_hl, pe_d, dve_o = sem("act_hh"), sem("dve_hl"), sem("pe_d"), sem("dve_o")
            dve_cur, dve_mask, pe_rank, dve_rank = sem("dve_cur"), sem("dve_mask"), sem("pe_rank"), sem("dve_rank")
            dve_ent, scattered = sem("dve_ent"), sem("scattered")
            steps = sem("route_steps")
            blk = tmp.enter_context(nc.Block())

            def rows(ap, q, t=None):
                if t is None:
                    return ap[bass.ds(q * TB, TB), :].rearrange("(t p) c -> p t c", p=P)
                return ap[bass.ds(q * TB + t * P, P), :]

            @blk.sync
            def _(sp):
                def load_x(q):
                    sp.dma_start(xin[:], rows(xf, q)).then_inc(x_ld, 16)

                def store_y(q):
                    for t in range(TT):
                        sp.wait_ge(act_yrow, TT * q + t + 1)
                        sp.dma_start(rows(y_rows, q, t), yrow[:, t % 2, :]).then_inc(y_st[t % 2], 16)

                def body(i, prep, more):
                    if some(16 * i):
                        sp.wait_ge(o_st, 16 * i)
                    sp.dma_start(xres[:], rows(xf, i)).then_inc(xres_ld, 16)
                    if prep:
                        store_y(i + 1)
                    if more:
                        sp.wait_ge(pe_tx, KC * (i + 2))
                        load_x(i + 2)
                    sp.wait_ge(dve_o, TT * (i + 1))
                    sp.dma_start(rows(acc, i), xres[:]).then_inc(o_st, 16)

                load_x(0)
                store_y(0)
                sp.wait_ge(pe_tx, KC)
                load_x(1)
                body(0, True, True)
                with sp.Fori(1, NBLK - 2) as i:
                    body(i, True, True)
                body(NBLK - 2, True, False)
                body(NBLK - 1, False, False)
                sp.wait_ge(o_st, 16 * NBLK)
                for q in range(2):
                    sp.wait_ge(y_st[q], 16 * NBLK * TT // 2)

            @blk.gpsimd
            def _(pool):
                def body(i):
                    for t in range(TT):
                        pool.wait_ge(dve_ent, TT * i + t + 1)
                        pool.nop(nofuse=True)
                        for k in range(TOPK):
                            nc.gpsimd.indirect_dma_start(
                                slots, bass.IndirectOffsetOnAxis(ap=pos[:, t, k:k + 1], axis=0),
                                ent[:, t, k, :], None).then_inc(scattered, 16)

                with pool.Fori(0, NBLK) as i:
                    body(i)
                pool.wait_ge(scattered, 16 * TOPK * TT * NBLK)

            @blk.tensor
            def _(pe):
                def products(dst, lhs, rhs, chunks, start=True, stop=True):
                    n = 0
                    for k in chunks:
                        for a, b in ((0, 0), (0, 1), (1, 0)):
                            last = nc.tensor.matmul(dst, lhs(a, k), rhs(b, k), start=start and n == 0,
                                                    stop=stop and n == 3 * len(chunks) - 1)
                            n += 1
                    return last

                def turn_x(q, k, first):
                    if k == 0:
                        pe.wait_ge(x_ld, 16 * (q + 1))
                        if not first:
                            if some(TT * q):
                                pe.wait_ge(act_yrow, TT * q)
                    elif k == 1:
                        if not first:
                            if some(q):
                                pe.wait_ge(act_sc, q)
                    else:
                        pe.wait_ge(dve_xtl, KC * q + k - 1)
                    for t in range(TT):
                        last = nc.tensor.transpose(misc[k % 2][:, t * P:(t + 1) * P], xin[:, t, k * P:(k + 1) * P], ident[:])
                    last.then_inc(pe_tx, 1)

                def make_y(q, m, first):
                    if m == 0:
                        pe.wait_ge(dve_xtl, KC * (q + 1))
                    elif m == 1:
                        if not first:
                            if some(q):
                                pe.wait_ge(dve_rank, q)
                    else:
                        pe.wait_ge(act_y, KC * q + m - 1)
                    products(misc[(m + 1) % 2][:], lambda a, k: wt[a][:, k, m * P:(m + 1) * P],
                             lambda b, k: xt[b][:, k, :], range(KC)).then_inc(pe_y, 1)

                def turn_y(q, t):
                    if t == 0:
                        pe.wait_ge(dve_y, KC * (q + 1))
                    elif t >= 2:
                        pe.wait_ge(act_yrow, TT * q + t - 1)
                    for k in range(KC):
                        last = nc.tensor.transpose(misc[(t + 1) % 2][:, k * P:(k + 1) * P], yt[:, k, t * P:(t + 1) * P], ident[:])
                    last.then_inc(pe_ty, 1)

                def route(q):
                    pe.wait_ge(act_yrow, TT * q + 3)
                    for t in range(TT):
                        for k in range(KC):
                            last = nc.tensor.matmul(misc[1][:, t * E:(t + 1) * E], yt[:, k, t * P:(t + 1) * P], rt[:, k, :],
                                                    start=(k == 0), stop=(k == KC - 1))
                    last.then_inc(pe_lg, 1)

                def ranks(i, prep):
                    if prep:
                        pe.wait_ge(dve_xtl, KC * (i + 1) + 3)
                    else:
                        pe.wait_ge(act_yrow, TT * NBLK)
                    pe.wait_ge(dve_mask, i + 1)
                    for t in range(TT + 1):
                        for s in range(min(t + 1, TT)):
                            last = nc.tensor.matmul(misc[0][:, t * E:(t + 1) * E], before[:] if s == t else ones[:], mask[:, s, :],
                                                    start=(s == 0), stop=(s == min(t, TT - 1)))
                    last.then_inc(pe_rank, 1)

                def gate(i, c):
                    if c == 0:
                        pe.wait_ge(dve_yl, KC * (i + 1))
                    if some(NCH * i + c):
                        pe.wait_ge(act_sg, NCH * i + c)
                    products(bg[:], lambda a, k: sgw[a][:, k, c * P:(c + 1) * P], lambda b, k: yp[b][:, k, :],
                             range(KC)).then_inc(pe_g, 1)

                def up(i, c):
                    if some(NCH * i + c):
                        pe.wait_ge(dve_h, NCH * i + c)
                    products(bu[:], lambda a, k: suw[a][:, k, c * P:(c + 1) * P], lambda b, k: yp[b][:, k, :],
                             range(KC)).then_inc(pe_u, 1)

                def down(i, c):
                    pe.wait_ge(dve_hl, NCH * i + c + 1)
                    if c == 0:
                        if some(TT * i):
                            pe.wait_ge(dve_o, TT * i)
                    for t in range(TT):
                        last = products(bo[t][:], lambda a, k: hp[a][:, c % 2, t * P:(t + 1) * P], lambda b, k: sdw[b][:, k, :],
                                        [c], start=(c == 0), stop=(c == NCH - 1))
                    last.then_inc(pe_d, 1)

                def body(i, prep):
                    for c in range(NCH):
                        gate(i, c)
                        up(i, c)
                        if c:
                            down(i, c - 1)
                        if prep and c in (0, 1):
                            turn_x(i + 1, 2 * c, False)
                            turn_x(i + 1, 2 * c + 1, False)
                        if c == 2:
                            ranks(i, prep)
                        if prep and c in (3, 4):
                            make_y(i + 1, 2 * (c - 3), False)
                            make_y(i + 1, 2 * (c - 3) + 1, False)
                        if prep and c in (5, 6):
                            turn_y(i + 1, 2 * (c - 5))
                            turn_y(i + 1, 2 * (c - 5) + 1)
                        if prep and c == 7:
                            route(i + 1)
                    down(i, NCH - 1)

                for k in range(KC):
                    turn_x(0, k, True)
                for m in range(KC):
                    make_y(0, m, True)
                for t in range(TT):
                    turn_y(0, t)
                route(0)
                body(0, True)
                with pe.Fori(1, NBLK - 1) as i:
                    body(i, True)
                body(NBLK - 1, False)

            @blk.scalar
            def _(act):
                def x_high(q, k):
                    act.wait_ge(pe_tx, KC * q + k + 1)
                    if k == 0:
                        act.wait_ge(dve_cur, q + 1)
                        if some(KC * q):
                            act.wait_ge(pe_y, KC * q)
                    nc.scalar.activation(xt[0][:, k, :], misc[k % 2][:], ACT.Copy, scale=cur[:, k:k + 1]).then_inc(act_xth, 1)

                def y_scale(q, m):
                    act.wait_ge(pe_y, KC * q + m + 1)
                    if m == 0:
                        if some(q):
                            act.wait_ge(pe_lg, q)
                        if some(KC * q):
                            act.wait_ge(dve_yl, KC * q)
                    nc.scalar.activation(yt[:, m, :], misc[(m + 1) % 2][:], ACT.Identity, scale=cur[:, KC + m:KC + m + 1],
                                         bias=bias_c[:, m:m + 1]).then_inc(act_y, 1)

                def y_row(q, t):
                    act.wait_ge(pe_ty, TT * q + t + 1)
                    if some(16 * (TT // 2 * q + t // 2)):
                        act.wait_ge(y_st[t % 2], 16 * (TT // 2 * q + t // 2))
                    nc.scalar.copy(yrow[:, t % 2, :], misc[(t + 1) % 2][:]).then_inc(act_yrow, 1)

                def y_high(q):
                    act.wait_ge(dve_y, KC * (q + 1))
                    if some(NCH * q):
                        act.wait_ge(pe_u, NCH * q)
                    for k in range(KC):
                        nc.scalar.copy(yp[0][:, k, :], yt[:, k, :]).then_inc(act_yh, 1)

                def scores(q):
                    act.wait_ge(pe_lg, q + 1)
                    if some(q):
                        act.wait_ge(dve_sc, q)
                    nc.scalar.activation(sc[:].rearrange("p t e -> p (t e)"), misc[1][:, 0:TT * E], ACT.Sigmoid).then_inc(act_sc, 1)

                def gate(i, c):
                    act.wait_ge(pe_g, NCH * i + c + 1)
                    if some(NCH * i + c):
                        act.wait_ge(dve_h, NCH * i + c)
                    nc.scalar.activation(sg[:], bg[:], ACT.Silu).then_inc(act_sg, 1)

                def h_high(i, c):
                    act.wait_ge(dve_h, NCH * i + c + 1)
                    if some(NCH * i + max(c - 1, 0)):
                        act.wait_ge(pe_d, NCH * i + max(c - 1, 0))
                    nc.scalar.copy(hp[0][:, c % 2, :], hf[:, c % 2, :]).then_inc(act_hh, 1)

                def body(i, prep):
                    for c in range(NCH):
                        gate(i, c)
                        h_high(i, c)
                        if prep and c in (0, 1):
                            x_high(i + 1, 2 * c)
                            x_high(i + 1, 2 * c + 1)
                        if prep and c in (3, 4):
                            y_scale(i + 1, 2 * (c - 3))
                            y_scale(i + 1, 2 * (c - 3) + 1)
                        if prep and c in (5, 6):
                            y_row(i + 1, 2 * (c - 5))
                            y_row(i + 1, 2 * (c - 5) + 1)
                    if prep:
                        y_high(i + 1)
                        scores(i + 1)

                for k in range(KC):
                    x_high(0, k)
                for m in range(KC):
                    y_scale(0, m)
                for t in range(TT):
                    y_row(0, t)
                y_high(0)
                scores(0)
                body(0, True)
                with act.Fori(1, NBLK - 1) as i:
                    body(i, True)
                body(NBLK - 1, False)

            STEPS = 20 + 3 * TT + 5 * TT

            @blk.vector
            def _(dve):
                def take_cur(q):
                    if some(KC * q):
                        dve.wait_ge(act_y, KC * q)
                    nc.vector.tensor_copy(cur[:], styles[:, bass.ds(q, 1), :].rearrange("p a k -> p (a k)")).then_inc(dve_cur, 1)

                def x_low(q, k):
                    dve.wait_ge(act_xth, KC * q + k + 1)
                    nc.vector.scalar_tensor_tensor(out=xt[1][:, k, :], in0=misc[k % 2][:], scalar=cur[:, k:k + 1],
                                                   in1=xt[0][:, k, :].bitcast(F32), op0=ALU.mult,
                                                   op1=ALU.subtract).then_inc(dve_xtl, 1)

                def y_clip(q, m):
                    dve.wait_ge(act_y, KC * q + m + 1)
                    nc.vector.tensor_scalar(yt[:, m, :], yt[:, m, :], CLAMP, -CLAMP, ALU.min, ALU.max).then_inc(dve_y, 1)

                def y_low(q):
                    for k in range(KC):
                        dve.wait_ge(act_yh, KC * q + k + 1)
                        sub_exact(nc, yp[1][:, k, :], yt[:, k, :], yp[0][:, k, :]).then_inc(dve_yl, 1)

                def hidden(i, c):
                    dve.wait_ge(act_sg, NCH * i + c + 1)
                    dve.wait_ge(pe_u, NCH * i + c + 1)
                    nc.vector.tensor_tensor(hf[:, c % 2, :], bu[:], sg[:], ALU.mult).then_inc(dve_h, 1)
                    dve.wait_ge(act_hh, NCH * i + c + 1)
                    sub_exact(nc, hp[1][:, c % 2, :], hf[:, c % 2, :], hp[0][:, c % 2, :]).then_inc(dve_hl, 1)

                def result(i):
                    dve.wait_ge(xres_ld, 16 * (i + 1))
                    dve.wait_ge(pe_d, NCH * (i + 1))
                    for t in range(TT):
                        nc.vector.tensor_tensor(xres[:, t, :], bo[t][:], xres[:, t, :], ALU.add).then_inc(dve_o, 1)

                flat = "p t e -> p (t e)"

                def by_group(ap):
                    return ap.rearrange("p t (g e) -> p t g e", g=GROUPS)

                def routing(i):
                    n = [0]

                    def link(ins):
                        n[0] += 1
                        ins.then_inc(steps, 1)
                        dve.wait_ge(steps, STEPS * i + n[0])

                    def grouped(ap):
                        return ap.rearrange("p t g -> p (t g)")

                    dve.wait_ge(act_sc, i + 1)
                    link(nc.vector.tensor_tensor(sbi[:], sc[:], eb[:].unsqueeze(1).to_broadcast([P, TT, E]), ALU.add))
                    link(nc.vector.tensor_reduce(g1[:], by_group(sbi[:]), AX_X, ALU.max))
                    link(nc.vector.tensor_tensor(by_group(t1[:]), by_group(sbi[:]),
                                                 g1[:].unsqueeze(3).to_broadcast([P, TT, GROUPS, EPG]), ALU.is_equal))
                    nc.vector.tensor_reduce(g2[:], by_group(t1[:]), AX_X, ALU.add)
                    link(nc.vector.scalar_tensor_tensor(out=t2[:], in0=t1[:], scalar=NEG, in1=sbi[:], op0=ALU.mult, op1=ALU.add))
                    nc.vector.tensor_reduce(g3[:], by_group(t2[:]), AX_X, ALU.max)
                    link(nc.vector.tensor_scalar(g2[:], g2[:], 1.5, NEG, ALU.is_lt, ALU.mult))
                    link(nc.vector.tensor_tensor(g2[:], g2[:], g1[:], ALU.add))
                    link(nc.vector.tensor_tensor(g2[:], g2[:], g3[:], ALU.max))
                    link(nc.vector.tensor_tensor(g1[:], g1[:], g2[:], ALU.add))
                    yield
                    mine = g1[:].unsqueeze(3).to_broadcast([P, TT, GROUPS, GROUPS])
                    theirs = g1[:].unsqueeze(2).to_broadcast([P, TT, GROUPS, GROUPS])
                    nc.vector.tensor_tensor(by_group(t1[:]), theirs, mine, ALU.is_equal)
                    link(nc.vector.tensor_tensor(by_group(t2[:]), theirs, mine, ALU.is_gt))
                    link(nc.vector.tensor_tensor(by_group(t1[:]), by_group(t1[:]),
                                                 lower[:].unsqueeze(1).to_broadcast([P, TT, GROUPS, GROUPS]), ALU.mult))
                    link(nc.vector.tensor_tensor(t1[:], t1[:], t2[:], ALU.add))
                    link(nc.vector.tensor_reduce(g2[:], by_group(t1[:]), AX_X, ALU.add))
                    link(nc.vector.tensor_scalar(g2[:], g2[:], TOPG - 0.5, NEG, ALU.is_gt, ALU.mult))
                    link(nc.vector.tensor_tensor(by_group(t1[:]), by_group(sbi[:]),
                                                 g2[:].unsqueeze(3).to_broadcast([P, TT, GROUPS, EPG]), ALU.add))
                    yield
                    for t in range(TT):
                        dve.nop(nofuse=True)
                        link(nc.vector.max(v8[:, t, :], t1[:, t, :]))
                        dve.nop(nofuse=True)
                        link(nc.vector.max_index(i8[:, t, :], v8[:, t, :], t1[:, t, :]))
                        dve.nop(nofuse=True)
                        link(nc.vector.match_replace(t2[:, t, :], v8[:, t, :], t1[:, t, :], TAKEN))
                    nc.vector.tensor_tensor(mask[:], t1[:], t2[:], ALU.not_equal).then_inc(dve_mask, 1)
                    dve.wait_ge(dve_mask, i + 1)
                    yield
                    link(nc.vector.tensor_tensor(wn[:], mask[:], sc[:], ALU.mult))
                    link(nc.vector.tensor_reduce(den[:], wn[:], AX_X, ALU.add))
                    nc.vector.tensor_copy(i8f[:], i8[:])
                    link(nc.vector.tensor_scalar(den[:], den[:], 1e-20, None, ALU.add))
                    nc.vector.reciprocal(rden[:], den[:]).then_inc(dve_sc, 1)
                    dve.wait_ge(pe_rank, i + 1)
                    ranked = misc[0][:, 0:TT * E].rearrange("p (t e) -> p t e", t=TT)
                    link(nc.vector.tensor_tensor(sl[:], ranked, base[:].unsqueeze(1).to_broadcast([P, TT, E]), ALU.add))
                    nc.vector.tensor_tensor(base[:], misc[0][:, TT * E:(TT + 1) * E], base[:], ALU.add).then_inc(dve_rank, 1)
                    if some(16 * TOPK * TT * i):
                        dve.wait_ge(scattered, 16 * TOPK * TT * i)
                    link(nc.vector.tensor_copy(ent[:, :, :, 0], tok[:].unsqueeze(2).to_broadcast([P, TT, TOPK])))
                    link(nc.vector.tensor_scalar(tok[:], tok[:], float(TB), None, ALU.add))
                    yield
                    for t in range(TT):
                        link(nc.vector.tensor_tensor(oh[:], iota_e[:].unsqueeze(1).to_broadcast([P, TOPK, E]),
                                                     i8f[:, t, :].unsqueeze(2).to_broadcast([P, TOPK, E]), ALU.is_equal))
                        link(nc.vector.tensor_tensor(oh2[:], oh[:], sl[:, t, :].unsqueeze(1).to_broadcast([P, TOPK, E]), ALU.mult))
                        link(nc.vector.tensor_reduce(pf[:, t, :], oh2[:], AX_X, ALU.add))
                        nc.vector.tensor_copy(pos[:, t, :], pf[:, t, :])
                        link(nc.vector.tensor_tensor(oh2[:], oh[:], wn[:, t, :].unsqueeze(1).to_broadcast([P, TOPK, E]), ALU.mult))
                        link(nc.vector.tensor_reduce(v8[:, t, :], oh2[:], AX_X, ALU.add))
                        nc.vector.tensor_scalar(ent[:, t, :, 1].bitcast(F32), v8[:, t, :], rden[:, t:t + 1], None,
                                                ALU.mult).then_inc(dve_ent, 1)
                        yield
                    assert n[0] == STEPS, n[0]

                pieces_of = {0: 2, 1: 1, 3: 1, 4: 1, 5: 2, 6: 2}

                def body(i, prep):
                    pieces = routing(i)
                    for c in range(NCH):
                        hidden(i, c)
                        if prep and c == 0:
                            take_cur(i + 1)
                        if prep and c in (0, 1):
                            x_low(i + 1, 2 * c)
                            x_low(i + 1, 2 * c + 1)
                        if c == 3:
                            next(pieces)
                        if prep and c in (3, 4):
                            y_clip(i + 1, 2 * (c - 3))
                            y_clip(i + 1, 2 * (c - 3) + 1)
                        if prep and c == NCH - 1:
                            y_low(i + 1)
                        if c != 3:
                            for _ in range(pieces_of.get(c, 0)):
                                next(pieces, None)
                    result(i)

                take_cur(0)
                for k in range(KC):
                    x_low(0, k)
                for m in range(KC):
                    y_clip(0, m)
                y_low(0)
                body(0, True)
                with dve.Fori(1, NBLK - 1) as i:
                    body(i, True)
                body(NBLK - 1, False)
        dense.close()

        RING = 4

        with ExitStack() as tmp:
            sb = sb_in(tmp)
            cnt = sb("cnt", [P, E])
            cnt_i = sb("cnt_i", [P, E], I32)
            tiles = sb("tiles", [P, E + 1])
            used = sb("used", [P, E + 1])
            one_e = sb("one_e", [P, E + 1])
            end = sb("end", [P, E + 1])
            nth = sb("nth", [P, E + 1])
            j_i = sb("j_i", [P, TQ], I32)
            jf = sb("jf", [P, TQ])
            past = sb("past", [P, TQ, E + 1])
            prod = sb("prod", [P, TQ, E + 1])
            eid, start, order, tmp_q = (sb(n, [P, TQ]) for n in ("eid", "start", "order", "tmp_q"))
            tab = sb("tab", [P, TQ, FLD], I32)
            j_made, tab_ok, tab_st = sem("j_made"), sem("tab_ok"), sem("tab_st")
            chain = sem("table_chain")
            blk = tmp.enter_context(nc.Block())

            @blk.gpsimd
            def _(pool):
                nc.gpsimd.iota(j_i[:], pattern=[[P, TQ]], base=0, channel_multiplier=1).then_inc(j_made, 1)

            @blk.vector
            def _(dve):
                n_link = [0]

                def link(ins):
                    n_link[0] += 1
                    ins.then_inc(chain, 1)
                    dve.wait_ge(chain, n_link[0])

                def over_tiles(ap):
                    return ap.unsqueeze(1).to_broadcast([P, TQ, E + 1])

                def over_experts(ap):
                    return ap.unsqueeze(2).to_broadcast([P, TQ, E + 1])

                nc.vector.memset(one_e[:], 1.0)
                nc.vector.memset(tiles[:, E:E + 1], float(TQ * P))
                nc.vector.memset(used[:, E:E + 1], 1.0)
                link(nc.vector.tensor_tensor(cnt[:], base[:], base0[:], ALU.subtract))
                nc.vector.tensor_scalar(used[:, 0:E], cnt[:], 0.5, None, ALU.is_gt)
                link(nc.vector.tensor_scalar(cnt_i[:], cnt[:], float(P - 1), None, ALU.add))
                link(nc.vector.tensor_scalar(cnt_i[:], cnt_i[:], LOG_P, None, ALU.arith_shift_right))
                link(nc.vector.tensor_copy(tiles[:, 0:E], cnt_i[:]))
                link(nc.vector.tensor_tensor_scan(end[:], one_e[:], tiles[:], 0.0, ALU.mult, ALU.add))
                nc.vector.tensor_tensor_scan(nth[:], one_e[:], used[:], 0.0, ALU.mult, ALU.add)
                dve.wait_ge(j_made, 1)
                link(nc.vector.tensor_copy(jf[:], j_i[:]))
                link(nc.vector.tensor_tensor(past[:], over_tiles(end[:]), over_experts(jf[:]), ALU.is_le))
                nc.vector.tensor_reduce(eid[:], past[:], AX_X, ALU.add)
                link(nc.vector.tensor_tensor(prod[:], past[:], over_tiles(tiles[:]), ALU.mult))
                link(nc.vector.tensor_reduce(start[:], prod[:], AX_X, ALU.add))
                link(nc.vector.tensor_tensor(prod[:], past[:], over_tiles(used[:]), ALU.mult))
                link(nc.vector.tensor_reduce(order[:], prod[:], AX_X, ALU.add))
                link(nc.vector.tensor_tensor(tmp_q[:], jf[:], start[:], ALU.subtract))
                link(nc.vector.tensor_scalar(tmp_q[:], tmp_q[:], float(P), None, ALU.mult))
                nc.vector.scalar_tensor_tensor(out=tab[:, :, 0], in0=eid[:], scalar=float(REG), in1=tmp_q[:],
                                               op0=ALU.mult, op1=ALU.add)
                nc.vector.tensor_copy(tab[:, :, 1], order[:])
                nc.vector.tensor_scalar(tab[:, :, 2], eid[:], float(E - 1), None, ALU.min)
                link(nc.vector.tensor_tensor(tab[:, :, 3], jf[:], start[:], ALU.is_equal))
                link(nc.vector.tensor_scalar(tmp_q[:], eid[:], E - 0.5, None, ALU.is_gt))
                link(nc.vector.tensor_tensor(tab[:, :, 6], tab[:, :, 3], tmp_q[:], ALU.max))
                link(nc.vector.tensor_scalar(tmp_q[:], order[:], -float(RING - 1), None, ALU.add))
                link(nc.vector.tensor_tensor(past[:], over_tiles(nth[:]), over_experts(tmp_q[:]), ALU.is_le))
                link(nc.vector.tensor_tensor(prod[:], past[:], over_tiles(tiles[:]), ALU.mult))
                link(nc.vector.tensor_reduce(start[:], prod[:], AX_X, ALU.add))
                nc.vector.tensor_copy(tab[:, :, 4], start[:])
                link(nc.vector.tensor_scalar(tab[:, :, 5], end[:, E - 1:E].to_broadcast([P, TQ]), -1.0, None, ALU.add))
                nc.vector.tensor_scalar(tab[:, :, 5], tab[:, :, 5], UN.bit_length() - 1, None,
                                        ALU.arith_shift_right).then_inc(tab_ok, 1)

            @blk.sync
            def _(sp):
                sp.wait_ge(tab_ok, 1)
                sp.dma_start(table.rearrange("(q p) f -> p q f", p=P), tab[:]).then_inc(tab_st, 16)
                sp.wait_ge(tab_st, 16)

        with ExitStack() as tmp:
            sb = sb_in(tmp)
            FIRSTS = UN + 2
            NWORD = MAXT // UN + 1
            trow = sb("trow", [1, TQ * P * FLD], I32)
            turns = sb("turns", [1, NWORD], I32)
            raw = [sb("raw_gu", [P, 2, KC, 2 * H]), sb("raw_d", [P, 2, KH, C])]
            wgu = [sb("w_gu_h", [P, RING, KC, 2 * H], F32R), sb("w_gu_l", [P, RING, KC, 2 * H], F32R)]
            wdn = [sb("w_dn_h", [P, RING, KH, C], F32R), sb("w_dn_l", [P, RING, KH, C], F32R)]
            lg = [sb(f"list_g{n}", [P, 2], I32) for n in range(UN)]
            ls = [sb(f"list_s{n}", [P, 2], I32) for n in range(UN)]
            xg = [sb(f"x_rows{n}", [P, C]) for n in range(UN)]
            xp = [sb("x_h", [P, 2, KC, P], F32R), sb("x_l", [P, 2, KC, P], F32R)]
            sg = sb("e_sg", [P, 2, H])
            hf = sb("e_hf", [P, 2, H])
            ident_r = sb("ident_r", [P, P], F32R)
            hp = [sb("e_h_h", [P, 2, KH, P], F32R), sb("e_h_l", [P, 2, KH, P], F32R)]
            og = [sb(f"o_rows{n}", [P, C]) for n in range(UN)]

            b_gu, b_x, b_h, b_o = bank[0:2], bank[2:4], bank[4:6], bank[6:8]

            tab_ld, raw_ld = sem("tab_ld"), sem("raw_ld")
            lg_ld = [sem(f"lg_ld{n}") for n in range(UN)]
            ls_ld = [sem(f"ls_ld{n}") for n in range(UN)]
            x_ld = [sem(f"x_rows_ld{n}") for n in range(UN)]
            added = [sem(f"added{n}") for n in range(UN)]
            SPLIT_0 = 4
            split = sem("split")
            w_high = sem("w_high")
            words, words_chain, ident_ok = sem("words"), sem("words_chain"), sem("ident_ok")
            pe_x, act_x, dve_x = sem("pe_x"), sem("act_x"), sem("dve_x")
            pe_gu, act_gu, dve_gu = sem("pe_gu"), sem("act_gu"), sem("dve_gu")
            pe_ht, act_ht, dve_ht = sem("pe_ht"), sem("act_ht"), sem("dve_ht")
            pe_do = sem("pe_do")
            act_do = sem("act_do")
            fin = sem("fin")
            blk = tmp.enter_context(nc.Block())

            PARTS = [(True, 0, KC // 2 + 1), (True, KC // 2 + 1, KC), (False, 0, KH)]
            NTURN = MAXT // UN
            assert MAXT % UN == 0 and NTURN > 2
            LAG_S = 5

            def field(eng, j, f, top_val):
                return eng.value_load(trow[0:1, bass.ds(j * FLD + f, 1)], min_val=0 if f != 5 else 4, max_val=top_val)

            class Turn:

                def __init__(self, eng, g):
                    self.word = eng.value_load(turns[0:1, bass.ds(g, 1)], min_val=0, max_val=((E + 1) << FIRSTS) - 1)

                def first(self, b):
                    return (self.word >> b) & 1

                def order(self, b):
                    n = self.word >> FIRSTS
                    for a in range(1, b + 1):
                        n = n + self.first(a)
                    return n

                def place(self, b):
                    if b < 0:
                        return ((self.word >> FIRSTS) + RING - self.first(0)) & (RING - 1)
                    return self.order(b) & (RING - 1)


            @blk.sync
            def _(sp):
                sp.dma_start(trow[:], table.rearrange("(a j) f -> a (j f)", a=1)).then_inc(tab_ld, 16)
                sp.wait_ge(tab_ld, 16)

                def load_list(dst, s, j):
                    off = field(sp, j, 0, LROWS - P)
                    sp.dma_start(dst[:], slots[bass.ds(off, P), :]).then_inc(s, 16)

                def weights(j):
                    with sp.If(field(sp, j, 3, 1) > 0):
                        order = field(sp, j, 1, E)
                        e = field(sp, j, 2, E - 1)
                        half = order & 1
                        sp.wait_ge(split, 3 * order + SPLIT_0 - 3)
                        sp.nop(nofuse=True)
                        if not isinstance(j, int) or j > 0:
                            sp.wait_ge(raw_ld, 48 * order)
                            sp.nop(nofuse=True)
                        for n, w in enumerate((gate_w, up_w)):
                            sp.dma_start(raw[0][:, bass.ds(half, 1), :, n * H:(n + 1) * H].rearrange("p a k n -> p (a k) n"),
                                         w[bass.ds(e, 1)].rearrange("e (k p) h -> p (e k) h", p=P)).then_inc(raw_ld, 16)
                        sp.dma_start(raw[1][:, bass.ds(half, 1), :, :].rearrange("p a k n -> p (a k) n"),
                                     down_w[bass.ds(e, 1)].rearrange("e (k p) h -> p (e k) h", p=P)).then_inc(raw_ld, 16)

                def step(g, u):
                    n = g * UN + u
                    known = isinstance(n, int)
                    if not known or n >= UN:
                        sp.wait_ge(x_ld[u], 16 * g)
                    load_list(lg[u], lg_ld[u], n)
                    if not known or n >= 1:
                        weights(n - 1)
                    if not known or n >= LAG_S:
                        m = n - LAG_S
                        if not known or m >= UN:
                            sp.wait_ge(added[(u - LAG_S) % UN], 16 * (g - (1 if u >= LAG_S - UN else 2)))
                        load_list(ls[(u - LAG_S) % UN], ls_ld[(u - LAG_S) % UN], m)

                for n in range(3 * UN):
                    step(n // UN, n % UN)
                last_turn = field(sp, 0, 5, NTURN - 1)
                with sp.Fori(3, NTURN + 1) as g:
                    with sp.If(last_turn >= g - 1):
                        for u in range(UN):
                            step(g, u)
                assert LAG_S == UN + 1
                sp.wait_ge(added[UN - 1], 16 * last_turn)
                load_list(ls[UN - 1], ls_ld[UN - 1], UN * last_turn + UN - 1)
                for u in range(UN):
                    sp.wait_ge(added[u], 16 * last_turn + 16)
                sp.dma_start(of, acc[0:N, :]).then_inc(fin, 16)
                sp.wait_ge(fin, 16)

            @blk.gpsimd
            def _(pool):
                def gather(g, u):
                    pool.wait_ge(lg_ld[u], 16 * (g + 1))
                    pool.nop(nofuse=True)
                    nc.gpsimd.indirect_dma_start(xg[u][:], None, y_rows,
                                                 bass.IndirectOffsetOnAxis(ap=lg[u][:, 0:1].bitcast(U32), axis=0)).then_inc(x_ld[u], 16)

                def scatter(m, u, gm):
                    pool.wait_ge(act_do, m + 1)
                    pool.wait_ge(ls_ld[u], 16 * (gm + 1))
                    with pool.If(field(pool, m, 6, 1) > 0):
                        for d in range(1, UN + 1):
                            done = gm + 1 if d <= u else gm
                            if d < UN and some(done):
                                pool.wait_ge(added[(u - d) % UN], 16 * done)
                        if some(gm):
                            pool.wait_ge(added[u], 16 * gm)
                    pool.nop(nofuse=True)
                    nc.gpsimd.indirect_dma_start(acc, bass.IndirectOffsetOnAxis(ap=ls[u][:, 0:1].bitcast(U32), axis=0),
                                                 og[u][:], None, compute_op=ALU.add).then_inc(added[u], 16)

                def step(g, u):
                    j = g * UN + u
                    pool.wait_ge(pe_x, j + 1)
                    gather(g + 1, u)
                    if not isinstance(j, int) or j >= 3:
                        scatter(j - 3, (u - 3) % UN, g - 1 if u < 3 else g)

                pool.wait_ge(tab_ld, 16)
                for u in range(UN):
                    gather(0, u)
                for u in range(UN):
                    step(0, u)
                for u in range(UN):
                    step(1, u)
                last_turn = field(pool, 0, 5, NTURN - 1)
                with pool.Fori(2, NTURN) as g:
                    with pool.If(last_turn >= g):
                        for u in range(UN):
                            step(g, u)
                for u in range(1, UN):
                    scatter(UN * last_turn + u, u, last_turn)
                for u in range(UN):
                    pool.wait_ge(x_ld[u], 16 * last_turn + 32)
                for u in range(UN):
                    pool.wait_ge(added[u], 16 * last_turn + 16)

            @blk.tensor
            def _(pe):
                pe.wait_ge(tab_ld, 16)
                pe.sem_inc(pe_do, 1)

                def turn_x(j, u, g):
                    if not isinstance(j, int) or j >= 2:
                        pe.wait_ge(dve_x, j - 1)
                    pe.wait_ge(x_ld[u], 16 * (g + 1))
                    for k in range(KC):
                        last = nc.tensor.transpose(b_x[u % 2][:, k * P:(k + 1) * P].bitcast(F32R),
                                                   xg[u][:, k * P:(k + 1) * P].bitcast(F32R), ident_r[:])
                    last.then_inc(pe_x, 1)

                def gate_up(j, u, place, chunks):
                    for k in chunks:
                        if k == 0:
                            if not isinstance(j, int) or j >= 2:
                                pe.wait_ge(dve_gu, j - 1)
                            pe.wait_ge(dve_x, j + 1)
                        for a, b in ((0, 0), (0, 1), (1, 0)):
                            last = nc.tensor.matmul(b_gu[u % 2][:], xp[a][:, u % 2, k, :],
                                                    wgu[b][:, bass.ds(place, 1), k, :].rearrange("p a n -> p (a n)"),
                                                    start=(k == 0 and a == b == 0), stop=(k == KC - 1 and a == 1))
                    if KC - 1 in chunks:
                        last.then_inc(pe_gu, 1)

                def turn_h(j, u):
                    if not isinstance(j, int) or j >= 2:
                        pe.wait_ge(dve_ht, j - 1)
                    pe.wait_ge(dve_gu, j + 1)
                    for k in range(KH):
                        last = nc.tensor.transpose(b_h[u % 2][:, k * P:(k + 1) * P],
                                                   hf[:, u % 2, k * P:(k + 1) * P].bitcast(F32), ident[:])
                    last.then_inc(pe_ht, 1)

                def down(j, u, place):
                    if not isinstance(j, int) or j >= 2:
                        pe.wait_ge(act_do, j - 1)
                    pe.wait_ge(dve_ht, j + 1)
                    for k in range(KH):
                        for a, b in ((0, 0), (0, 1), (1, 0)):
                            last = nc.tensor.matmul(b_o[u % 2][:], hp[a][:, u % 2, k, :],
                                                    wdn[b][:, bass.ds(place, 1), k, :].rearrange("p a n -> p (a n)"),
                                                    start=(k == 0 and a == b == 0), stop=(k == KH - 1 and a == 1))
                    last.then_inc(pe_do, 1)

                def step(g, u, turn):
                    j = g * UN + u
                    before_it = not isinstance(j, int) or j >= 1
                    turn_x(j + 1, (u + 1) % UN, g + 1 if u == UN - 1 else g)
                    place = turn.place(u)
                    pe.wait_ge(split, 3 * turn.order(u) + 3 + SPLIT_0)
                    gate_up(j, u, place, range(0, 1))
                    if before_it:
                        turn_h(j - 1, (u - 1) % UN)
                    gate_up(j, u, place, range(1, KC))
                    if before_it:
                        down(j - 1, (u - 1) % UN, turn.place(u - 1))

                pe.wait_ge(ident_ok, 1)
                pe.wait_ge(words, 1)
                turn_x(0, 0, 0)
                for g in range(2):
                    turn = Turn(pe, g)
                    for u in range(UN):
                        step(g, u, turn)
                last_turn = field(pe, 0, 5, NTURN - 1)
                with pe.Fori(2, NTURN) as g:
                    with pe.If(last_turn >= g):
                        turn = Turn(pe, g)
                        for u in range(UN):
                            step(g, u, turn)
                end = UN * last_turn + UN - 1
                turn_h(end, UN - 1)
                down(end, UN - 1, field(pe, end, 1, E) & (RING - 1))

            @blk.scalar
            def _(act):
                act.wait_ge(tab_ld, 16)

                def x_high(j, u):
                    act.wait_ge(pe_x, j + 1)
                    if not isinstance(j, int) or j >= 2:
                        act.wait_ge(pe_gu, j - 1)
                    nc.scalar.copy(xp[0][:, u % 2, :, :].rearrange("p k t -> p (k t)"), b_x[u % 2][:]).then_inc(act_x, 1)

                def silu(j, u):
                    act.wait_ge(pe_gu, j + 1)
                    if not isinstance(j, int) or j >= 2:
                        act.wait_ge(dve_gu, j - 1)
                    nc.scalar.activation(sg[:, u % 2, :], b_gu[u % 2][:, 0:H], ACT.Silu).then_inc(act_gu, 1)

                def h_high(j, u):
                    act.wait_ge(pe_ht, j + 1)
                    if not isinstance(j, int) or j >= 2:
                        act.wait_ge(pe_do, j)
                    nc.scalar.copy(hp[0][:, u % 2, :, :].rearrange("p k t -> p (k t)"), b_h[u % 2][:, 0:H]).then_inc(act_ht, 1)

                def weigh(j, u, g):
                    act.wait_ge(pe_do, j + 2)
                    act.wait_ge(ls_ld[u], 16 * (g + 1))
                    if not isinstance(j, int) or j >= UN:
                        act.wait_ge(added[u], 16 * g)
                    nc.scalar.activation(og[u][:], b_o[u % 2][:], ACT.Copy, scale=ls[u][:, 1:2].bitcast(F32)).then_inc(act_do, 1)

                def weights_high(order, half, place, part):
                    gu, k0, k1 = PARTS[part]
                    nc.scalar.copy((wgu if gu else wdn)[0][:, bass.ds(place, 1), k0:k1, :].rearrange("p a k n -> p (a k n)"),
                                   raw[0 if gu else 1][:, bass.ds(half, 1), k0:k1, :].rearrange("p a k n -> p (a k n)")
                                   ).then_inc(w_high, 1)

                def start_weights(j, order):
                    if j is not None:
                        act.wait_ge(pe_do, field(act, j, 4, MAXT) + 1)
                    act.wait_ge(raw_ld, 48 * order + 48)
                    weights_high(order, order & 1, order & (RING - 1), 0)

                def end_weights(order):
                    for part in (1, 2):
                        weights_high(order, order & 1, order & (RING - 1), part)

                def step(g, u, turn):
                    j = g * UN + u
                    known = isinstance(j, int)
                    x_high(j + 1, (u + 1) % UN)
                    if not known or j >= 2:
                        weigh(j - 2, (u - 2) % UN, g - 1 if u < 2 else g)
                    if not known or j >= 1:
                        h_high(j - 1, (u - 1) % UN)
                    with act.If(turn.first(u + 2) > 0):
                        start_weights(j + 2, turn.order(u + 2))
                    silu(j, u)
                    with act.If(turn.first(u + 2) > 0):
                        end_weights(turn.order(u + 2))

                act.wait_ge(words, 1)
                start_weights(None, 0)
                end_weights(0)
                x_high(0, 0)
                turn = Turn(act, 0)
                with act.If(turn.first(1) > 0):
                    start_weights(None, turn.order(1))
                    end_weights(turn.order(1))
                for u in range(UN):
                    step(0, u, turn)
                turn = Turn(act, 1)
                for u in range(UN):
                    step(1, u, turn)
                last_turn = field(act, 0, 5, NTURN - 1)
                with act.Fori(2, NTURN) as g:
                    with act.If(last_turn >= g):
                        turn = Turn(act, g)
                        for u in range(UN):
                            step(g, u, turn)
                end = UN * last_turn + UN - 1
                weigh(UN * last_turn + UN - 2, UN - 2, last_turn)
                h_high(end, UN - 1)
                weigh(end, UN - 1, last_turn)

            @blk.vector
            def _(dve):
                dve.wait_ge(tab_ld, 16)
                dve.sem_inc(split, SPLIT_0)
                nc.vector.tensor_copy(ident_r[:], ident[:]).then_inc(ident_ok, 1)

                def x_low(j, u):
                    dve.wait_ge(act_x, j + 1)
                    sub_exact(nc, xp[1][:, u % 2, :, :].rearrange("p k t -> p (k t)"), b_x[u % 2][:],
                              xp[0][:, u % 2, :, :].rearrange("p k t -> p (k t)")).then_inc(dve_x, 1)

                def hidden(j, u):
                    dve.wait_ge(act_gu, j + 1)
                    if not isinstance(j, int) or j >= 2:
                        dve.wait_ge(pe_ht, j - 1)
                    nc.vector.tensor_tensor(hf[:, u % 2, :], b_gu[u % 2][:, H:2 * H], sg[:, u % 2, :], ALU.mult).then_inc(dve_gu, 1)

                def h_low(j, u):
                    dve.wait_ge(act_ht, j + 1)
                    sub_exact(nc, hp[1][:, u % 2, :, :].rearrange("p k t -> p (k t)"), b_h[u % 2][:, 0:H],
                              hp[0][:, u % 2, :, :].rearrange("p k t -> p (k t)")).then_inc(dve_ht, 1)

                def weights_low(order, parts):
                    half, place = order & 1, order & (RING - 1)
                    dve.wait_ge(w_high, 3 * order + parts[-1] + 1)
                    for part in parts:
                        gu, k0, k1 = PARTS[part]
                        w = wgu if gu else wdn
                        sub_exact(nc, w[1][:, bass.ds(place, 1), k0:k1, :].rearrange("p a k n -> p (a k n)"),
                                  raw[0 if gu else 1][:, bass.ds(half, 1), k0:k1, :].rearrange("p a k n -> p (a k n)"),
                                  w[0][:, bass.ds(place, 1), k0:k1, :].rearrange("p a k n -> p (a k n)")).then_inc(split, 1)

                def step(g, u, turn):
                    j = g * UN + u
                    x_low(j + 1, (u + 1) % UN)
                    if not isinstance(j, int) or j >= 1:
                        h_low(j - 1, (u - 1) % UN)
                    with dve.If(turn.first(u + 1) > 0):
                        weights_low(turn.order(u + 1), (1, 2))
                    hidden(j, u)
                    with dve.If(turn.first(u + 2) > 0):
                        weights_low(turn.order(u + 2), (0,))

                def of_turns(b, f):
                    return trow[0:1, b * FLD + f:(b + (NWORD - 1) * UN) * FLD + f + 1:UN * FLD]

                n_link = [0]

                def link(ins):
                    n_link[0] += 1
                    ins.then_inc(words_chain, 1)
                    dve.wait_ge(words_chain, n_link[0])

                link(nc.vector.tensor_copy(turns[:], of_turns(FIRSTS - 1, 3)))
                for b in range(FIRSTS - 2, -1, -1):
                    link(nc.vector.scalar_tensor_tensor(out=turns[:], in0=turns[:], scalar=2.0, in1=of_turns(b, 3),
                                                        op0=ALU.mult, op1=ALU.add))
                nc.vector.scalar_tensor_tensor(out=turns[:], in0=of_turns(0, 1), scalar=float(1 << FIRSTS), in1=turns[:],
                                               op0=ALU.mult, op1=ALU.add).then_inc(words, 1)
                dve.wait_ge(words, 1)
                weights_low(0, (0, 1, 2))
                x_low(0, 0)
                turn = Turn(dve, 0)
                with dve.If(turn.first(1) > 0):
                    weights_low(turn.order(1), (0,))
                for u in range(UN):
                    step(0, u, turn)
                turn = Turn(dve, 1)
                for u in range(UN):
                    step(1, u, turn)
                last_turn = field(dve, 0, 5, NTURN - 1)
                with dve.Fori(2, NTURN) as g:
                    with dve.If(last_turn >= g):
                        turn = Turn(dve, g)
                        for u in range(UN):
                            step(g, u, turn)
                h_low(UN * last_turn + UN - 1, UN - 1)


_INS = ['x', 'cond_512', 'L0_cond_weight', 'L0_cond_bias', 'L0_cond_affine_w', 'L0_cond_affine_b', 'L0_ffn_router_w',
        'L0_ffn_e_bias', 'L0_ffn_gate_w', 'L0_ffn_up_w', 'L0_ffn_down_w', 'L0_ffn_sh_gate_w', 'L0_ffn_sh_up_w',
        'L0_ffn_sh_down_w']
_OUTS = [((8, 1024, 512), 'float32')]


def kernel(**inputs):
    import numpy as _np
    import concourse.bacc as _bacc
    from concourse import mybir as _mybir
    from concourse.bass_utils import run_bass_kernel_spmd as _run

    nc = _bacc.Bacc("TRN2", target_bir_lowering=False, num_devices=1)
    arrays, args = {}, []
    for name in _INS:
        a = _np.ascontiguousarray(inputs[name])
        arrays[f"in_{name}_dram"] = a
        args.append(nc.dram_tensor(f"in_{name}_dram", a.shape, _mybir.dt.from_np(a.dtype), kind="ExternalInput").ap())
    for i, (shape, dtype) in enumerate(_OUTS):
        dt = _mybir.dt.from_np(_np.dtype(dtype))
        args.append(nc.dram_tensor(f"out_{i}_dram", shape, dt, kind="ExternalOutput").ap())
    build(nc, *args)
    r = _run(nc, [arrays], core_ids=[0])
    got = tuple(r.results[0][f"out_{i}_dram"] for i in range(len(_OUTS)))
    return got[0]
```

```python
from contextlib import ExitStack

import concourse.bass as bass
import numpy as np
from concourse import mybir

ALU = mybir.AluOpType
ACT = mybir.ActivationFunctionType
AX_X = mybir.AxisListType.X
F32 = mybir.dt.float32
F32R = mybir.dt.float32r
BF16 = mybir.dt.bfloat16
I32 = mybir.dt.int32
U32 = mybir.dt.uint32

P = 128

NEG = -3.0e38
TAKEN = -3.3e38


def some(n):
    return not isinstance(n, int) or n > 0


def sub_exact(nc, out, full, high):
    return nc.vector.tensor_tensor(out, full, high.bitcast(F32), ALU.subtract)


def build(nc, x, cond, cw, cbias, aff_w, aff_b, router_w, e_bias, gate_w, up_w, down_w,
          sh_gate, sh_up, sh_down, out):
    B, L, C = x.shape
    N = B * L
    WD = cond.shape[1]
    E, _, H = gate_w.shape
    HS = sh_gate.shape[1]
    TOPK, GROUPS, TOPG = 8, 8, 4
    EPG = E // GROUPS
    CLAMP = 256.0
    KC = C // P
    KH = H // P
    KW = WD // P
    TB = 512
    TT = TB // P
    NBLK = N // TB
    NCH = HS // P
    LOG_P = P.bit_length() - 1
    MAXT = N * TOPK // P + E
    UN = 4
    TQ = -(-(MAXT + 2 * UN) // P)
    REG = N
    LROWS = -(-(E * REG + TQ * P * P) // (P * P)) * P * P
    RING = 4
    FLD = 7

    xf = x.rearrange("b l c -> (b l) c")
    assert tuple(out.shape) == (N + P, C)
    y_rows = nc.dram_tensor("y_rows", (N + P, C), F32).ap()
    slots = nc.dram_tensor("slot_list", (LROWS, 2), I32).ap()
    table = nc.dram_tensor("tile_table", (TQ * P, FLD), I32).ap()

    top = ExitStack()

    def sem(name):
        return top.enter_context(nc.semaphore(name))

    with top:
        keep = ExitStack()
        top.enter_context(keep)

        def sb_in(stack):
            return lambda name, shape, dt=F32: stack.enter_context(nc.sbuf_tensor(name, shape, dt))

        bank = [top.enter_context(nc.psum_tensor(f"bank{n}", [P, 512], F32)) for n in range(8)]

        sb = sb_in(keep)
        ident = sb("ident", [P, P])
        base = sb("base", [P, E])
        base0 = sb("base0", [P, E])
        zrow = sb("zrow", [P, C])

        dense = ExitStack()
        sb = sb_in(dense)
        sgw = [sb("sh_gate_h", [P, KC, HS], F32R), sb("sh_gate_l", [P, KC, HS], F32R)]
        suw = [sb("sh_up_h", [P, KC, HS], F32R), sb("sh_up_l", [P, KC, HS], F32R)]
        sdw = [sb("sh_down_h", [P, NCH, C], F32R), sb("sh_down_l", [P, NCH, C], F32R)]
        wt = [sb("w_h", [P, KC, C], F32R), sb("w_l", [P, KC, C], F32R)]
        rt = sb("router_t", [P, KC, E])
        bias_c = sb("bias_c", [P, KC])
        styles = sb("styles", [P, NBLK, 2 * KC])
        eb = sb("e_bias_b", [P, E])
        before = sb("before", [P, P], BF16)
        ones = sb("ones", [P, P], BF16)
        iota_e = sb("iota_e", [P, E])
        lower = sb("lower", [P, GROUPS, GROUPS])
        tok = sb("tok", [P, TT], I32)
        pad = sb("pad", [P, P, 2], I32)
        tab = sb("tab", [P, TQ, FLD], I32)
        j_i = sb("j_i", [P, TQ], I32)
        xin = sb("xin", [P, TT, C])
        made, zeroed, filled, high = sem("made"), sem("zeroed"), sem("filled"), sem("high")
        x_ld = sem("x_ld")
        ld_sh = [sem("ld_sh_gate"), sem("ld_sh_up"), sem("ld_sh_down")]
        stage_d = sb("stage_d", [P, NCH, C])
        xres = stage_d[:, 0:TT, :]
        assert NCH == TT + 4 and TOPK * E == C == TB
        oh, oh2 = (stage_d[:, TT + n, :].rearrange("p (k e) -> p k e", e=E) for n in range(2))
        hf = stage_d[:, TT + 2:TT + 4, :]

        with ExitStack() as tmp:
            sb = sb_in(tmp)
            stage = [sb("stage_g", [P, KC, HS]), sb("stage_u", [P, KC, HS]), stage_d]
            w_raw = sb("w_raw", [P, KC, C])
            aw_raw = sb("aw_raw", [P, KC, WD])
            rw_raw = sb("rw_raw", [E, C])
            cond_raw = sb("cond_raw", [B, WD])
            ab = sb("ab", [P, KC])
            cond_t = sb("cond_t", [P, KW, B])
            aw_t = sb("aw_t", [P, KW, C])
            w_sq = sb("w_sq", [P, KC, C])
            st = sb("st", [P, KC, B])
            st_sq = sb("st_sq", [P, KC, B])
            dco = sb("dco", [P, KC, B])
            sq_sum = sb("sq_sum", [P, KC, B])
            root = sb("root", [P, KC, B])
            iota_i = sb("iota_i", [P, E], I32)
            low_i = sb("low_i", [P, GROUPS, GROUPS], I32)

            ld_small, ld_w, ld_aff, ld_r = sem("ld_small"), sem("ld_w"), sem("ld_aff"), sem("ld_r")
            turned = sem("turned")
            copied = sem("copied")
            squared = sem("squared")
            low = sem("low")
            st_mm, st_ok, sq_mm = sem("st_mm"), sem("st_ok"), sem("sq_mm")
            chain = sem("setup_chain")
            rooted = sem("rooted")
            ROOT_AT = 6
            blk = tmp.enter_context(nc.Block())

            @blk.sync
            def _(sp):
                sp.dma_start(aw_raw[:], aff_w.rearrange("(k p) w -> p k w", p=P)).then_inc(ld_aff, 16)
                sp.dma_start(cond_raw[:], cond).then_inc(ld_aff, 16)
                sp.dma_start(w_raw[:], cw.rearrange("(k p) c -> p k c", p=P)).then_inc(ld_w, 16)
                sp.dma_start(rw_raw[:], router_w).then_inc(ld_r, 16)
                with nc.allow_non_contiguous_dma(reason="small columns"):
                    sp.dma_start(ab[:], aff_b.rearrange("(k p) -> p k", p=P)).then_inc(ld_small, 16)
                    sp.dma_start(bias_c[:], cbias.rearrange("(k p) -> p k", p=P)).then_inc(ld_small, 16)
                sp.dma_start(eb[:], e_bias.partition_broadcast(P)).then_inc(ld_small, 16)
                for n, w in enumerate((sh_gate, sh_up, sh_down)):
                    if n == 1:
                        sp.dma_start(xin[:], xf[0:TB, :].rearrange("(t p) c -> p t c", p=P)).then_inc(x_ld, 16)
                    sp.dma_start(stage[n][:], w.rearrange("(k p) h -> p k h", p=P)).then_inc(ld_sh[n], 16)

            @blk.gpsimd
            def _(pool):
                nc.gpsimd.memset(ident[:], 0.0).then_inc(made, 1)
                pool.wait_ge(made, 1)
                nc.gpsimd.affine_select(out=ident[:], in_=ident[:], compare_op=ALU.not_equal, fill=1.0,
                                        base=0, pattern=[[-1, P]], channel_multiplier=1).then_inc(made, 1)
                nc.gpsimd.memset(ones[:], 1.0).then_inc(made, 1)
                pool.wait_ge(made, 3)
                nc.gpsimd.affine_select(out=before[:], in_=ones[:], compare_op=ALU.is_gt, fill=0.0,
                                        base=0, pattern=[[1, P]], channel_multiplier=-1).then_inc(made, 1)
                nc.gpsimd.memset(pad[:], 0).then_inc(made, 1)
                nc.gpsimd.iota(iota_i[:], pattern=[[1, E]], base=0, channel_multiplier=0).then_inc(made, 1)
                pool.wait_ge(made, 6)
                nc.gpsimd.iota(pad[:, :, 0:1].rearrange("p r k -> p (r k)"), pattern=[[1, P]], base=N,
                               channel_multiplier=0).then_inc(made, 1)
                nc.gpsimd.iota(low_i[:], pattern=[[1, GROUPS], [-1, GROUPS]], base=0,
                               channel_multiplier=0).then_inc(made, 1)
                nc.gpsimd.iota(tok[:], pattern=[[P, TT]], base=0, channel_multiplier=1).then_inc(made, 1)
                nc.gpsimd.iota(j_i[:], pattern=[[P, TQ]], base=0, channel_multiplier=1).then_inc(made, 1)
                pool.wait_ge(high, KC + 2)
                nc.gpsimd.tensor_tensor(suw[1][:, 0:KC // 2, :], stage[1][:, 0:KC // 2, :],
                                        suw[0][:, 0:KC // 2, :].bitcast(F32), ALU.subtract)
                pool.wait_ge(ld_sh[2], 16)

            @blk.tensor
            def _(pe):
                pe.wait_ge(made, 2)
                pe.wait_ge(ld_aff, 32)
                for k in range(KW):
                    nc.tensor.transpose(bank[0][:, k * B:(k + 1) * B], cond_raw[:, k * P:(k + 1) * P], ident[0:B, 0:B])
                for k in range(KW):
                    for m in range(KC):
                        last = nc.tensor.transpose(bank[1 + k][:, m * P:(m + 1) * P], aw_raw[:, m, k * P:(k + 1) * P], ident[:])
                last.then_inc(turned, 1)
                pe.wait_ge(ld_r, 16)
                for k in range(KC):
                    last = nc.tensor.transpose(bank[3][:, k * E:(k + 1) * E], rw_raw[:, k * P:(k + 1) * P], ident[0:E, 0:E])
                last.then_inc(turned, 1)
                pe.wait_ge(ld_w, 16)
                for k in range(KC):
                    for m in range(KC):
                        last = nc.tensor.transpose(bank[4 + k][:, m * P:(m + 1) * P], w_raw[:, m, k * P:(k + 1) * P], ident[:])
                    last.then_inc(turned, 1)
                pe.wait_ge(copied, 2)
                for m in range(KC):
                    for k in range(KW):
                        last = nc.tensor.matmul(bank[0][:, 64 + m * B:64 + (m + 1) * B], aw_t[:, k, m * P:(m + 1) * P],
                                                cond_t[:, k, :], start=(k == 0), stop=(k == KW - 1))
                last.then_inc(st_mm, 1)
                pe.wait_ge(st_ok, 1)
                pe.wait_ge(squared, KC)
                for m in range(KC):
                    for k in range(KC):
                        last = nc.tensor.matmul(bank[1][:, m * B:(m + 1) * B], w_sq[:, k, m * P:(m + 1) * P],
                                                st_sq[:, k, :], start=(k == 0), stop=(k == KC - 1))
                last.then_inc(sq_mm, 1)

            @blk.scalar
            def _(act):
                for k in range(KC):
                    act.wait_ge(turned, 3 + k)
                    nc.scalar.copy(wt[0][:, k, :], bank[4 + k][:]).then_inc(high, 1)
                    nc.scalar.activation(w_sq[:, k, :], bank[4 + k][:], ACT.Square).then_inc(squared, 1)
                act.wait_ge(ld_sh[0], 16)
                nc.scalar.copy(sgw[0][:], stage[0][:]).then_inc(high, 1)
                act.wait_ge(ld_sh[1], 16)
                nc.scalar.copy(suw[0][:], stage[1][:]).then_inc(high, 1)
                act.wait_ge(chain, ROOT_AT)
                nc.scalar.activation(root[:], sq_sum[:], ACT.Sqrt).then_inc(rooted, 1)

            @blk.vector
            def _(dve):
                n_link = [0]

                def link(ins):
                    n_link[0] += 1
                    ins.then_inc(chain, 1)
                    dve.wait_ge(chain, n_link[0])

                nc.vector.memset(zrow[:], 0.0).then_inc(zeroed, 1)
                dve.wait_ge(made, 10)
                link(nc.vector.tensor_copy(iota_e[:], iota_i[:]))
                link(nc.vector.tensor_scalar(base[:], iota_e[:], float(REG), None, ALU.mult))
                link(nc.vector.tensor_copy(base0[:], base[:]))
                link(nc.vector.tensor_scalar(lower[:], low_i[:], 0.0, None, ALU.is_gt))
                dve.wait_ge(turned, 1)
                nc.vector.tensor_copy(cond_t[:].rearrange("p k b -> p (k b)"), bank[0][:, 0:KW * B])
                for k in range(KW):
                    last = nc.vector.tensor_copy(aw_t[:, k, :], bank[1 + k][:])
                    if k == KW - 1:
                        last.then_inc(copied, 1)
                dve.wait_ge(turned, 2)
                nc.vector.tensor_copy(rt[:].rearrange("p k e -> p (k e)"), bank[3][:, 0:KC * E]).then_inc(copied, 1)
                dve.wait_ge(st_mm, 1)
                dve.wait_ge(ld_small, 48)
                gain = float(WD) ** -0.5
                for m in range(KC):
                    last = nc.vector.tensor_scalar(st[:, m, :], bank[0][:, 64 + m * B:64 + (m + 1) * B], gain, ab[:, m:m + 1],
                                                   ALU.mult, ALU.add)
                link(last)
                nc.vector.tensor_tensor(st_sq[:], st[:], st[:], ALU.mult).then_inc(st_ok, 1)
                for k in range(KC):
                    dve.wait_ge(squared, k + 1)
                    sub_exact(nc, wt[1][:, k, :], bank[4 + k][:], wt[0][:, k, :])
                dve.wait_ge(high, KC + 1)
                sub_exact(nc, sgw[1][:], stage[0][:], sgw[0][:])
                dve.wait_ge(sq_mm, 1)
                flat_d = "p k b -> p (k b)"
                link(nc.vector.tensor_scalar(sq_sum[:].rearrange(flat_d), bank[1][:, 0:KC * B], 1e-8, None, ALU.add))
                dve.wait_ge(rooted, 1)
                link(nc.vector.reciprocal(dco[:], root[:]))
                link(nc.vector.tensor_tensor(root[:], dco[:], dco[:], ALU.mult))
                link(nc.vector.tensor_tensor(root[:], root[:], sq_sum[:], ALU.mult))
                link(nc.vector.tensor_scalar(root[:], root[:], -0.5, 1.5, ALU.mult, ALU.add))
                link(nc.vector.tensor_tensor(dco[:], dco[:], root[:], ALU.mult))
                per = NBLK // B
                for h in range(per):
                    v = styles[:].rearrange("p (b h) k -> p h k b", h=per)[:, h]
                    nc.vector.tensor_copy(v[:, 0:KC, :], st[:])
                    link(nc.vector.tensor_copy(v[:, KC:2 * KC, :], dco[:]))
                dve.wait_ge(high, KC + 2)
                sub_exact(nc, suw[1][:, KC // 2:KC, :], stage[1][:, KC // 2:KC, :], suw[0][:, KC // 2:KC, :])

        with ExitStack() as tmp:
            sb = sb_in(tmp)
            xt = [sb("xt_h", [P, KC, TB], F32R), sb("xt_l", [P, KC, TB], F32R)]
            yt = sb("yt", [P, KC, TB])
            yp = [sb("y_h", [P, KC, TB], F32R), sb("y_l", [P, KC, TB], F32R)]
            yrow = sb("yrow", [P, 2, C])
            cur = sb("cur", [P, 2 * KC])
            sg = sb("sg", [P, TB])
            hp = [sb("h_h", [P, 2, TB], F32R), sb("h_l", [P, 2, TB], F32R)]
            sc = sb("sc", [P, TT, E])
            sbi = sb("sbi", [P, TT, E])
            t1 = sb("t1", [P, TT, E])
            t2 = sb("t2", [P, TT, E])
            mask = sb("mask", [P, TT, E], BF16)
            wn = sb("wn", [P, TT, E])
            sl = sb("sl", [P, TT, E])
            g1, g2, g3 = (sb(f"g{n}", [P, TT, GROUPS]) for n in range(3))
            v8 = sb("v8", [P, TT, TOPK])
            i8 = sb("i8", [P, TT, TOPK], U32)
            i8f = sb("i8f", [P, TT, TOPK])
            pf = sb("pf", [P, TT, TOPK])
            pos = sb("pos", [P, TT, TOPK], U32)
            ent = sb("ent", [P, TT, TOPK, 2], I32)
            den = sb("den", [P, TT])
            rden = sb("rden", [P, TT])

            bg, bu = bank[0], bank[1]
            bo = bank[2:6]
            misc = bank[6:8]

            xres_ld, o_st = sem("xres_ld"), sem("o_st")
            y_st = [sem("y_st0"), sem("y_st1")]
            pe_tx, act_xth, dve_xtl = sem("pe_tx"), sem("act_xth"), sem("dve_xtl")
            pe_y, act_y, dve_y = sem("pe_y"), sem("act_y"), sem("dve_y")
            pe_ty, act_yrow = sem("pe_ty"), sem("act_yrow")
            act_yh, dve_yl = sem("act_yh"), sem("dve_yl")
            pe_lg, act_sc, dve_sc = sem("pe_lg"), sem("act_sc"), sem("dve_sc")
            pe_g, act_sg, pe_u, dve_h = sem("pe_g"), sem("act_sg"), sem("pe_u"), sem("dve_h")
            act_hh, dve_hl, pe_d, dve_o = sem("act_hh"), sem("dve_hl"), sem("pe_d"), sem("dve_o")
            dve_cur, dve_mask, pe_rank, dve_rank = sem("dve_cur"), sem("dve_mask"), sem("pe_rank"), sem("dve_rank")
            dve_ent, scattered = sem("dve_ent"), sem("scattered")
            tab_ok, tab_st, table_chain = sem("tab_ok"), sem("tab_st"), sem("table_chain")
            pool_split = sem("pool_split")
            steps = sem("route_steps")
            blk = tmp.enter_context(nc.Block())

            def rows(ap, q, t=None):
                if t is None:
                    return ap[bass.ds(q * TB, TB), :].rearrange("(t p) c -> p t c", p=P)
                return ap[bass.ds(q * TB + t * P, P), :]

            @blk.sync
            def _(sp):
                def load_x(q):
                    sp.dma_start(xin[:], rows(xf, q)).then_inc(x_ld, 16)

                def store_y(q):
                    for t in range(TT):
                        sp.wait_ge(act_yrow, TT * q + t + 1)
                        sp.dma_start(rows(y_rows, q, t), yrow[:, t % 2, :]).then_inc(y_st[t % 2], 16)

                def body(i, prep, more):
                    if isinstance(i, int) and i == 0:
                        sp.wait_ge(pool_split, 2)
                    if some(16 * i):
                        sp.wait_ge(o_st, 16 * i)
                    sp.dma_start(xres[:], rows(xf, i)).then_inc(xres_ld, 16)
                    if prep:
                        store_y(i + 1)
                    if more:
                        sp.wait_ge(pe_tx, KC * (i + 2))
                        load_x(i + 2)
                    sp.wait_ge(dve_o, TT * (i + 1))
                    sp.dma_start(rows(out, i), xres[:]).then_inc(o_st, 16)

                sp.wait_ge(made, 7)
                sp.wait_ge(zeroed, 1)
                per = LROWS // P // P
                sp.dma_start(slots.rearrange("(q a r) k -> q a (r k)", q=P, a=per),
                             pad[:].rearrange("p r k -> p (r k)").unsqueeze(1).to_broadcast([P, per, 2 * P])
                             ).then_inc(filled, 16)
                sp.dma_start(y_rows[N:N + P, :], zrow[:]).then_inc(filled, 16)
                sp.dma_start(out[N:N + P, :], zrow[:]).then_inc(filled, 16)
                sp.wait_ge(pe_tx, KC)
                load_x(1)
                store_y(0)
                body(0, True, True)
                with sp.Fori(1, NBLK - 2) as i:
                    body(i, True, True)
                body(NBLK - 2, True, False)
                body(NBLK - 1, False, False)
                sp.wait_ge(tab_ok, 1)
                sp.dma_start(table.rearrange("(q p) f -> p q f", p=P), tab[:]).then_inc(tab_st, 16)
                sp.wait_ge(tab_st, 16)
                sp.wait_ge(o_st, 16 * NBLK)
                for q in range(2):
                    sp.wait_ge(y_st[q], 16 * NBLK * TT // 2)

            @blk.gpsimd
            def _(pool):
                def body(i):
                    for t in range(TT):
                        pool.wait_ge(dve_ent, TT * i + t + 1)
                        pool.nop(nofuse=True)
                        for k in range(TOPK):
                            nc.gpsimd.indirect_dma_start(
                                slots, bass.IndirectOffsetOnAxis(ap=pos[:, t, k:k + 1], axis=0),
                                ent[:, t, k, :], None).then_inc(scattered, 16)

                nc.gpsimd.tensor_copy(sdw[0][:], stage_d[:]).then_inc(pool_split, 1)
                pool.wait_ge(pool_split, 1)
                nc.gpsimd.tensor_tensor(sdw[1][:], stage_d[:], sdw[0][:].bitcast(F32), ALU.subtract).then_inc(pool_split, 1)
                pool.wait_ge(filled, 48)
                with pool.Fori(0, NBLK) as i:
                    body(i)
                pool.wait_ge(scattered, 16 * TOPK * TT * NBLK)

            @blk.tensor
            def _(pe):
                def products(dst, lhs, rhs, chunks, start=True, stop=True):
                    n = 0
                    for k in chunks:
                        for a, b in ((0, 0), (0, 1), (1, 0)):
                            last = nc.tensor.matmul(dst, lhs(a, k), rhs(b, k), start=start and n == 0,
                                                    stop=stop and n == 3 * len(chunks) - 1)
                            n += 1
                    return last

                def turn_x(q, k, first):
                    if k == 0:
                        pe.wait_ge(x_ld, 16 * (q + 1))
                        if not first:
                            if some(TT * q):
                                pe.wait_ge(act_yrow, TT * q)
                    elif k == 1:
                        if not first:
                            if some(q):
                                pe.wait_ge(act_sc, q)
                    else:
                        pe.wait_ge(dve_xtl, KC * q + k - 1)
                    for t in range(TT):
                        last = nc.tensor.transpose(misc[k % 2][:, t * P:(t + 1) * P], xin[:, t, k * P:(k + 1) * P], ident[:])
                    last.then_inc(pe_tx, 1)

                def make_y(q, m, first):
                    if m == 0:
                        pe.wait_ge(dve_xtl, KC * (q + 1))
                    elif m == 1:
                        if not first:
                            if some(q):
                                pe.wait_ge(dve_rank, q)
                    else:
                        pe.wait_ge(act_y, KC * q + m - 1)
                    products(misc[(m + 1) % 2][:], lambda a, k: wt[a][:, k, m * P:(m + 1) * P],
                             lambda b, k: xt[b][:, k, :], range(KC)).then_inc(pe_y, 1)

                def turn_y(q, t):
                    if t == 0:
                        pe.wait_ge(dve_y, KC * (q + 1))
                    elif t >= 2:
                        pe.wait_ge(act_yrow, TT * q + t - 1)
                    for k in range(KC):
                        last = nc.tensor.transpose(misc[(t + 1) % 2][:, k * P:(k + 1) * P], yt[:, k, t * P:(t + 1) * P], ident[:])
                    last.then_inc(pe_ty, 1)

                def route(q):
                    pe.wait_ge(act_yrow, TT * q + 3)
                    for t in range(TT):
                        for k in range(KC):
                            last = nc.tensor.matmul(misc[1][:, t * E:(t + 1) * E], yt[:, k, t * P:(t + 1) * P], rt[:, k, :],
                                                    start=(k == 0), stop=(k == KC - 1))
                    last.then_inc(pe_lg, 1)

                def ranks(i, prep):
                    if prep:
                        pe.wait_ge(dve_xtl, KC * (i + 1) + 3)
                    else:
                        pe.wait_ge(act_yrow, TT * NBLK)
                    pe.wait_ge(dve_mask, i + 1)
                    for t in range(TT + 1):
                        for s in range(min(t + 1, TT)):
                            last = nc.tensor.matmul(misc[0][:, t * E:(t + 1) * E], before[:] if s == t else ones[:], mask[:, s, :],
                                                    start=(s == 0), stop=(s == min(t, TT - 1)))
                    last.then_inc(pe_rank, 1)

                def gate(i, c):
                    if c == 0:
                        pe.wait_ge(dve_yl, KC * (i + 1))
                    if some(NCH * i + c):
                        pe.wait_ge(act_sg, NCH * i + c)
                    products(bg[:], lambda a, k: sgw[a][:, k, c * P:(c + 1) * P], lambda b, k: yp[b][:, k, :],
                             range(KC)).then_inc(pe_g, 1)

                def up(i, c):
                    if some(NCH * i + c):
                        pe.wait_ge(dve_h, NCH * i + c)
                    products(bu[:], lambda a, k: suw[a][:, k, c * P:(c + 1) * P], lambda b, k: yp[b][:, k, :],
                             range(KC)).then_inc(pe_u, 1)

                def down(i, c):
                    pe.wait_ge(dve_hl, NCH * i + c + 1)
                    if c == 0:
                        if isinstance(i, int) and i == 0:
                            pe.wait_ge(pool_split, 2)
                        if some(TT * i):
                            pe.wait_ge(dve_o, TT * i)
                    for t in range(TT):
                        last = products(bo[t][:], lambda a, k: hp[a][:, c % 2, t * P:(t + 1) * P], lambda b, k: sdw[b][:, k, :],
                                        [c], start=(c == 0), stop=(c == NCH - 1))
                    last.then_inc(pe_d, 1)

                def body(i, prep):
                    for c in range(NCH):
                        gate(i, c)
                        up(i, c)
                        if c == (3 if prep else 2):
                            ranks(i, prep)
                        if c:
                            down(i, c - 1)
                        if prep and c in (0, 1):
                            turn_x(i + 1, 2 * c, False)
                            turn_x(i + 1, 2 * c + 1, False)
                        if prep and c in (3, 4):
                            make_y(i + 1, 2 * (c - 3), False)
                            make_y(i + 1, 2 * (c - 3) + 1, False)
                        if prep and c in (5, 6):
                            turn_y(i + 1, 2 * (c - 5))
                            turn_y(i + 1, 2 * (c - 5) + 1)
                        if prep and c == 7:
                            route(i + 1)
                    down(i, NCH - 1)

                for k in range(KC):
                    turn_x(0, k, True)
                for m in range(KC):
                    make_y(0, m, True)
                for t in range(TT):
                    turn_y(0, t)
                route(0)
                body(0, True)
                with pe.Fori(1, NBLK - 1) as i:
                    body(i, True)
                body(NBLK - 1, False)

            @blk.scalar
            def _(act):
                def x_high(q, k):
                    act.wait_ge(pe_tx, KC * q + k + 1)
                    if k == 0:
                        act.wait_ge(dve_cur, q + 1)
                        if some(KC * q):
                            act.wait_ge(pe_y, KC * q)
                    nc.scalar.activation(xt[0][:, k, :], misc[k % 2][:], ACT.Copy, scale=cur[:, k:k + 1]).then_inc(act_xth, 1)

                def y_scale(q, m):
                    act.wait_ge(pe_y, KC * q + m + 1)
                    if m == 0:
                        if some(q):
                            act.wait_ge(pe_lg, q)
                        if some(KC * q):
                            act.wait_ge(dve_yl, KC * q)
                    nc.scalar.activation(yt[:, m, :], misc[(m + 1) % 2][:], ACT.Identity, scale=cur[:, KC + m:KC + m + 1],
                                         bias=bias_c[:, m:m + 1]).then_inc(act_y, 1)

                def y_row(q, t):
                    act.wait_ge(pe_ty, TT * q + t + 1)
                    if some(16 * (TT // 2 * q + t // 2)):
                        act.wait_ge(y_st[t % 2], 16 * (TT // 2 * q + t // 2))
                    nc.scalar.copy(yrow[:, t % 2, :], misc[(t + 1) % 2][:]).then_inc(act_yrow, 1)

                def y_high(q):
                    act.wait_ge(dve_y, KC * (q + 1))
                    if some(NCH * q):
                        act.wait_ge(pe_u, NCH * q)
                    for k in range(KC):
                        nc.scalar.copy(yp[0][:, k, :], yt[:, k, :]).then_inc(act_yh, 1)

                def scores(q):
                    act.wait_ge(pe_lg, q + 1)
                    if some(q):
                        act.wait_ge(dve_sc, q)
                    nc.scalar.activation(sc[:].rearrange("p t e -> p (t e)"), misc[1][:, 0:TT * E], ACT.Sigmoid).then_inc(act_sc, 1)

                def gate(i, c):
                    act.wait_ge(pe_g, NCH * i + c + 1)
                    if some(NCH * i + c):
                        act.wait_ge(dve_h, NCH * i + c)
                    nc.scalar.activation(sg[:], bg[:], ACT.Silu).then_inc(act_sg, 1)

                def h_high(i, c):
                    act.wait_ge(dve_h, NCH * i + c + 1)
                    if some(NCH * i + max(c - 1, 0)):
                        act.wait_ge(pe_d, NCH * i + max(c - 1, 0))
                    nc.scalar.copy(hp[0][:, c % 2, :], hf[:, c % 2, :]).then_inc(act_hh, 1)

                def body(i, prep):
                    for c in range(NCH):
                        gate(i, c)
                        h_high(i, c)
                        if prep and c in (0, 1):
                            x_high(i + 1, 2 * c)
                            x_high(i + 1, 2 * c + 1)
                        if prep and c in (3, 4):
                            y_scale(i + 1, 2 * (c - 3))
                            y_scale(i + 1, 2 * (c - 3) + 1)
                        if prep and c in (5, 6):
                            y_row(i + 1, 2 * (c - 5))
                            y_row(i + 1, 2 * (c - 5) + 1)
                    if prep:
                        y_high(i + 1)
                        scores(i + 1)

                for k in range(KC):
                    x_high(0, k)
                for m in range(KC):
                    y_scale(0, m)
                for t in range(TT):
                    y_row(0, t)
                y_high(0)
                scores(0)
                body(0, True)
                with act.Fori(1, NBLK - 1) as i:
                    body(i, True)
                body(NBLK - 1, False)

            STEPS = 20 + 3 * TT + 5 * TT

            @blk.vector
            def _(dve):
                def take_cur(q):
                    if some(KC * q):
                        dve.wait_ge(act_y, KC * q)
                    nc.vector.tensor_copy(cur[:], styles[:, bass.ds(q, 1), :].rearrange("p a k -> p (a k)")).then_inc(dve_cur, 1)

                def x_low(q, k):
                    dve.wait_ge(act_xth, KC * q + k + 1)
                    nc.vector.scalar_tensor_tensor(out=xt[1][:, k, :], in0=misc[k % 2][:], scalar=cur[:, k:k + 1],
                                                   in1=xt[0][:, k, :].bitcast(F32), op0=ALU.mult,
                                                   op1=ALU.subtract).then_inc(dve_xtl, 1)

                def y_clip(q, m):
                    dve.wait_ge(act_y, KC * q + m + 1)
                    nc.vector.tensor_scalar(yt[:, m, :], yt[:, m, :], CLAMP, -CLAMP, ALU.min, ALU.max).then_inc(dve_y, 1)

                def y_low(q):
                    for k in range(KC):
                        dve.wait_ge(act_yh, KC * q + k + 1)
                        sub_exact(nc, yp[1][:, k, :], yt[:, k, :], yp[0][:, k, :]).then_inc(dve_yl, 1)

                def hidden(i, c):
                    if isinstance(i, int) and i == c == 0:
                        dve.wait_ge(pool_split, 2)
                    dve.wait_ge(act_sg, NCH * i + c + 1)
                    dve.wait_ge(pe_u, NCH * i + c + 1)
                    nc.vector.tensor_tensor(hf[:, c % 2, :], bu[:], sg[:], ALU.mult).then_inc(dve_h, 1)
                    dve.wait_ge(act_hh, NCH * i + c + 1)
                    sub_exact(nc, hp[1][:, c % 2, :], hf[:, c % 2, :], hp[0][:, c % 2, :]).then_inc(dve_hl, 1)

                def result(i):
                    dve.wait_ge(xres_ld, 16 * (i + 1))
                    dve.wait_ge(pe_d, NCH * (i + 1))
                    for t in range(TT):
                        nc.vector.tensor_tensor(xres[:, t, :], bo[t][:], xres[:, t, :], ALU.add).then_inc(dve_o, 1)

                flat = "p t e -> p (t e)"

                def by_group(ap):
                    return ap.rearrange("p t (g e) -> p t g e", g=GROUPS)

                def routing(i):
                    n = [0]

                    def link(ins):
                        n[0] += 1
                        ins.then_inc(steps, 1)
                        dve.wait_ge(steps, STEPS * i + n[0])

                    def grouped(ap):
                        return ap.rearrange("p t g -> p (t g)")

                    dve.wait_ge(act_sc, i + 1)
                    link(nc.vector.tensor_tensor(sbi[:], sc[:], eb[:].unsqueeze(1).to_broadcast([P, TT, E]), ALU.add))
                    link(nc.vector.tensor_reduce(g1[:], by_group(sbi[:]), AX_X, ALU.max))
                    link(nc.vector.tensor_tensor(by_group(t1[:]), by_group(sbi[:]),
                                                 g1[:].unsqueeze(3).to_broadcast([P, TT, GROUPS, EPG]), ALU.is_equal))
                    nc.vector.tensor_reduce(g2[:], by_group(t1[:]), AX_X, ALU.add)
                    link(nc.vector.scalar_tensor_tensor(out=t2[:], in0=t1[:], scalar=NEG, in1=sbi[:], op0=ALU.mult, op1=ALU.add))
                    nc.vector.tensor_reduce(g3[:], by_group(t2[:]), AX_X, ALU.max)
                    link(nc.vector.tensor_scalar(g2[:], g2[:], 1.5, NEG, ALU.is_lt, ALU.mult))
                    link(nc.vector.tensor_tensor(g2[:], g2[:], g1[:], ALU.add))
                    link(nc.vector.tensor_tensor(g2[:], g2[:], g3[:], ALU.max))
                    link(nc.vector.tensor_tensor(g1[:], g1[:], g2[:], ALU.add))
                    yield
                    mine = g1[:].unsqueeze(3).to_broadcast([P, TT, GROUPS, GROUPS])
                    theirs = g1[:].unsqueeze(2).to_broadcast([P, TT, GROUPS, GROUPS])
                    nc.vector.tensor_tensor(by_group(t1[:]), theirs, mine, ALU.is_equal)
                    link(nc.vector.tensor_tensor(by_group(t2[:]), theirs, mine, ALU.is_gt))
                    link(nc.vector.tensor_tensor(by_group(t1[:]), by_group(t1[:]),
                                                 lower[:].unsqueeze(1).to_broadcast([P, TT, GROUPS, GROUPS]), ALU.mult))
                    link(nc.vector.tensor_tensor(t1[:], t1[:], t2[:], ALU.add))
                    link(nc.vector.tensor_reduce(g2[:], by_group(t1[:]), AX_X, ALU.add))
                    link(nc.vector.tensor_scalar(g2[:], g2[:], TOPG - 0.5, NEG, ALU.is_gt, ALU.mult))
                    link(nc.vector.tensor_tensor(by_group(t1[:]), by_group(sbi[:]),
                                                 g2[:].unsqueeze(3).to_broadcast([P, TT, GROUPS, EPG]), ALU.add))
                    yield
                    for t in range(TT):
                        dve.nop(nofuse=True)
                        link(nc.vector.max(v8[:, t, :], t1[:, t, :]))
                        dve.nop(nofuse=True)
                        link(nc.vector.max_index(i8[:, t, :], v8[:, t, :], t1[:, t, :]))
                        dve.nop(nofuse=True)
                        link(nc.vector.match_replace(t2[:, t, :], v8[:, t, :], t1[:, t, :], TAKEN))
                    nc.vector.tensor_tensor(mask[:], t1[:], t2[:], ALU.not_equal).then_inc(dve_mask, 1)
                    dve.wait_ge(dve_mask, i + 1)
                    yield
                    link(nc.vector.tensor_tensor(wn[:], mask[:], sc[:], ALU.mult))
                    link(nc.vector.tensor_reduce(den[:], wn[:], AX_X, ALU.add))
                    nc.vector.tensor_copy(i8f[:], i8[:])
                    link(nc.vector.tensor_scalar(den[:], den[:], 1e-20, None, ALU.add))
                    nc.vector.reciprocal(rden[:], den[:]).then_inc(dve_sc, 1)
                    dve.wait_ge(pe_rank, i + 1)
                    ranked = misc[0][:, 0:TT * E].rearrange("p (t e) -> p t e", t=TT)
                    link(nc.vector.tensor_tensor(sl[:], ranked, base[:].unsqueeze(1).to_broadcast([P, TT, E]), ALU.add))
                    nc.vector.tensor_tensor(base[:], misc[0][:, TT * E:(TT + 1) * E], base[:], ALU.add).then_inc(dve_rank, 1)
                    if some(16 * TOPK * TT * i):
                        dve.wait_ge(scattered, 16 * TOPK * TT * i)
                    link(nc.vector.tensor_copy(ent[:, :, :, 0], tok[:].unsqueeze(2).to_broadcast([P, TT, TOPK])))
                    link(nc.vector.tensor_scalar(tok[:], tok[:], float(TB), None, ALU.add))
                    yield
                    for t in range(TT):
                        link(nc.vector.tensor_tensor(oh[:], iota_e[:].unsqueeze(1).to_broadcast([P, TOPK, E]),
                                                     i8f[:, t, :].unsqueeze(2).to_broadcast([P, TOPK, E]), ALU.is_equal))
                        link(nc.vector.tensor_tensor(oh2[:], oh[:], sl[:, t, :].unsqueeze(1).to_broadcast([P, TOPK, E]), ALU.mult))
                        link(nc.vector.tensor_reduce(pf[:, t, :], oh2[:], AX_X, ALU.add))
                        nc.vector.tensor_copy(pos[:, t, :], pf[:, t, :])
                        link(nc.vector.tensor_tensor(oh2[:], oh[:], wn[:, t, :].unsqueeze(1).to_broadcast([P, TOPK, E]), ALU.mult))
                        link(nc.vector.tensor_reduce(v8[:, t, :], oh2[:], AX_X, ALU.add))
                        nc.vector.tensor_scalar(ent[:, t, :, 1].bitcast(F32), v8[:, t, :], rden[:, t:t + 1], None,
                                                ALU.mult).then_inc(dve_ent, 1)
                        yield
                    assert n[0] == STEPS, n[0]

                pieces_of = {0: 2, 1: 1, 3: 1, 4: 1, 5: 2, 6: 2}
                pieces_of_last = {0: 3, 2: 2, 3: 2, 4: 2}

                def body(i, prep):
                    pieces = routing(i)
                    for c in range(NCH):
                        hidden(i, c)
                        if prep and c == 0:
                            take_cur(i + 1)
                        if prep and c in (0, 1):
                            x_low(i + 1, 2 * c)
                            x_low(i + 1, 2 * c + 1)
                        if prep and c == 3:
                            next(pieces)
                        if prep and c in (3, 4):
                            y_clip(i + 1, 2 * (c - 3))
                            y_clip(i + 1, 2 * (c - 3) + 1)
                        if prep and c == NCH - 1:
                            y_low(i + 1)
                        if not prep or c != 3:
                            for _ in range((pieces_of if prep else pieces_of_last).get(c, 0)):
                                next(pieces, None)
                        if not prep and c == 5:
                            make_table()
                    result(i)

                def make_table():
                    at = [0]

                    def small(shape, dt=F32):
                        n = int(np.prod(shape))
                        v = xin[:].rearrange("p t c -> p (t c)")[:, at[0]:at[0] + n]
                        at[0] += n
                        if dt is not F32:
                            v = v.bitcast(dt)
                        return v if len(shape) == 1 else v.rearrange("p (a b) -> p a b", b=shape[-1])

                    cnt, cnt_i = small([E]), small([E], I32)
                    tiles, used, one_e, end = (small([E + 1]) for _ in range(4))
                    nth = small([E + 1])
                    past, prod = small([TQ, E + 1]), small([TQ, E + 1])
                    jf, eid, start, order, tmp_q = (small([TQ]) for _ in range(5))
                    n_link = [0]

                    def link(ins):
                        n_link[0] += 1
                        ins.then_inc(table_chain, 1)
                        dve.wait_ge(table_chain, n_link[0])

                    def over_tiles(ap):
                        return ap.unsqueeze(1).to_broadcast([P, TQ, E + 1])

                    def over_experts(ap):
                        return ap.unsqueeze(2).to_broadcast([P, TQ, E + 1])

                    dve.wait_ge(dve_rank, NBLK)
                    nc.vector.memset(one_e, 1.0)
                    nc.vector.memset(tiles[:, E:E + 1], float(TQ * P))
                    nc.vector.memset(used[:, E:E + 1], 1.0)
                    link(nc.vector.tensor_tensor(cnt, base[:], base0[:], ALU.subtract))
                    nc.vector.tensor_scalar(used[:, 0:E], cnt, 0.5, None, ALU.is_gt)
                    link(nc.vector.tensor_scalar(cnt_i, cnt, float(P - 1), None, ALU.add))
                    link(nc.vector.tensor_scalar(cnt_i, cnt_i, LOG_P, None, ALU.arith_shift_right))
                    link(nc.vector.tensor_copy(tiles[:, 0:E], cnt_i))
                    link(nc.vector.tensor_tensor_scan(end, one_e, tiles, 0.0, ALU.mult, ALU.add))
                    nc.vector.tensor_tensor_scan(nth, one_e, used, 0.0, ALU.mult, ALU.add)
                    link(nc.vector.tensor_copy(jf, j_i[:]))
                    link(nc.vector.tensor_tensor(past, over_tiles(end), over_experts(jf), ALU.is_le))
                    nc.vector.tensor_reduce(eid, past, AX_X, ALU.add)
                    link(nc.vector.tensor_tensor(prod, past, over_tiles(tiles), ALU.mult))
                    link(nc.vector.tensor_reduce(start, prod, AX_X, ALU.add))
                    link(nc.vector.tensor_tensor(prod, past, over_tiles(used), ALU.mult))
                    link(nc.vector.tensor_reduce(order, prod, AX_X, ALU.add))
                    link(nc.vector.tensor_tensor(tmp_q, jf, start, ALU.subtract))
                    link(nc.vector.tensor_scalar(tmp_q, tmp_q, float(P), None, ALU.mult))
                    nc.vector.scalar_tensor_tensor(out=tab[:, :, 0], in0=eid, scalar=float(REG), in1=tmp_q,
                                                   op0=ALU.mult, op1=ALU.add)
                    nc.vector.tensor_copy(tab[:, :, 1], order)
                    nc.vector.tensor_scalar(tab[:, :, 2], eid, float(E - 1), None, ALU.min)
                    link(nc.vector.tensor_tensor(tab[:, :, 3], jf, start, ALU.is_equal))
                    link(nc.vector.tensor_scalar(tmp_q, eid, E - 0.5, None, ALU.is_gt))
                    link(nc.vector.tensor_tensor(tab[:, :, 6], tab[:, :, 3], tmp_q, ALU.max))
                    link(nc.vector.tensor_scalar(tmp_q, order, -float(RING - 1), None, ALU.add))
                    link(nc.vector.tensor_tensor(past, over_tiles(nth), over_experts(tmp_q), ALU.is_le))
                    link(nc.vector.tensor_tensor(prod, past, over_tiles(tiles), ALU.mult))
                    link(nc.vector.tensor_reduce(start, prod, AX_X, ALU.add))
                    nc.vector.tensor_copy(tab[:, :, 4], start)
                    link(nc.vector.tensor_scalar(tab[:, :, 5], end[:, E - 1:E].to_broadcast([P, TQ]), -1.0, None, ALU.add))
                    nc.vector.tensor_scalar(tab[:, :, 5], tab[:, :, 5], UN.bit_length() - 1, None,
                                            ALU.arith_shift_right).then_inc(tab_ok, 1)

                take_cur(0)
                for k in range(KC):
                    x_low(0, k)
                for m in range(KC):
                    y_clip(0, m)
                y_low(0)
                body(0, True)
                with dve.Fori(1, NBLK - 1) as i:
                    body(i, True)
                body(NBLK - 1, False)
        dense.close()


        with ExitStack() as tmp:
            sb = sb_in(tmp)
            FIRSTS = UN + 3
            NWORD = MAXT // UN + 1
            trow = sb("trow", [1, TQ * P * FLD], I32)
            turns = sb("turns", [1, NWORD], I32)
            raw = [sb("raw_gu", [P, 2, KC, 2 * H]), sb("raw_d", [P, 2, KH, C])]
            wgu = [sb("w_gu_h", [P, RING, KC, 2 * H], F32R), sb("w_gu_l", [P, RING, KC, 2 * H], F32R)]
            wdn = [sb("w_dn_h", [P, RING, KH, C], F32R), sb("w_dn_l", [P, RING, KH, C], F32R)]
            lg = [sb(f"list_g{n}", [P, 2], I32) for n in range(UN)]
            ls = [sb(f"list_s{n}", [P, 2], I32) for n in range(UN)]
            xg = [sb(f"x_rows{n}", [P, C]) for n in range(UN)]
            xp = [sb("x_h", [P, 2, KC, P], F32R), sb("x_l", [P, 2, KC, P], F32R)]
            sg = sb("e_sg", [P, 2, H])
            hf = sb("e_hf", [P, 2, H])
            ident_r = sb("ident_r", [P, P], F32R)
            hp = [sb("e_h_h", [P, 2, KH, P], F32R), sb("e_h_l", [P, 2, KH, P], F32R)]
            og = [sb(f"o_rows{n}", [P, C]) for n in range(UN)]

            b_gu, b_x, b_h, b_o = bank[0:2], bank[2:4], bank[4:6], bank[6:8]

            tab_ld = sem("tab_ld")
            raw_gu_ld, raw_d_ld = sem("raw_gu_ld"), sem("raw_d_ld")
            lg_ld = [sem(f"lg_ld{n}") for n in range(UN)]
            ls_ld = [sem(f"ls_ld{n}") for n in range(UN)]
            x_ld = [sem(f"x_rows_ld{n}") for n in range(UN)]
            added = [sem(f"added{n}") for n in range(UN)]
            SPLIT_0 = 4
            split = sem("split")
            w_high = sem("w_high")
            words, words_chain, ident_ok = sem("words"), sem("words_chain"), sem("ident_ok")
            pe_x, act_x, dve_x = sem("pe_x"), sem("act_x"), sem("dve_x")
            pe_gu, act_gu, dve_gu = sem("pe_gu"), sem("act_gu"), sem("dve_gu")
            pe_ht, act_ht, dve_ht = sem("pe_ht"), sem("act_ht"), sem("dve_ht")
            pe_do = sem("pe_do")
            act_do = sem("act_do")
            blk = tmp.enter_context(nc.Block())

            PARTS = [(True, 0, KC // 2 + 1), (True, KC // 2 + 1, KC), (False, 0, KH)]
            NTURN = MAXT // UN
            assert MAXT % UN == 0 and NTURN > 2
            LAG_S = 5

            def field(eng, j, f, top_val):
                return eng.value_load(trow[0:1, bass.ds(j * FLD + f, 1)], min_val=0 if f != 5 else 4, max_val=top_val)

            class Turn:

                def __init__(self, eng, g):
                    self.word = eng.value_load(turns[0:1, bass.ds(g, 1)], min_val=0, max_val=((E + 1) << FIRSTS) - 1)

                def first(self, b):
                    return (self.word >> (b + 1)) & 1

                def order(self, b):
                    n = self.word >> FIRSTS
                    for a in range(1, b + 1):
                        n = n + self.first(a)
                    return n

                def place(self, b):
                    if b < 0:
                        n = (self.word >> FIRSTS) + RING
                        for a in range(b + 1, 1):
                            n = n - self.first(a)
                        return n & (RING - 1)
                    return self.order(b) & (RING - 1)


            @blk.sync
            def _(sp):
                sp.dma_start(trow[:], table.rearrange("(a j) f -> a (j f)", a=1)).then_inc(tab_ld, 16)
                sp.wait_ge(tab_ld, 16)

                def load_list(dst, s, j):
                    off = field(sp, j, 0, LROWS - P)
                    sp.dma_start(dst[:], slots[bass.ds(off, P), :]).then_inc(s, 16)

                def weights(j):
                    with sp.If(field(sp, j, 3, 1) > 0):
                        order = field(sp, j, 1, E)
                        e = field(sp, j, 2, E - 1)
                        half = order & 1
                        sp.wait_ge(split, 3 * order + SPLIT_0 - 3)
                        sp.nop(nofuse=True)
                        if not isinstance(j, int) or j > 0:
                            sp.wait_ge(raw_gu_ld, 32 * order)
                            sp.nop(nofuse=True)
                            sp.wait_ge(raw_d_ld, 16 * order)
                            sp.nop(nofuse=True)
                        for n, w in enumerate((gate_w, up_w)):
                            sp.dma_start(raw[0][:, bass.ds(half, 1), :, n * H:(n + 1) * H].rearrange("p a k n -> p (a k) n"),
                                         w[bass.ds(e, 1)].rearrange("e (k p) h -> p (e k) h", p=P)).then_inc(raw_gu_ld, 16)
                        sp.dma_start(raw[1][:, bass.ds(half, 1), :, :].rearrange("p a k n -> p (a k) n"),
                                     down_w[bass.ds(e, 1)].rearrange("e (k p) h -> p (e k) h", p=P)).then_inc(raw_d_ld, 16)

                def step(g, u):
                    n = g * UN + u
                    known = isinstance(n, int)
                    if not known or n >= UN:
                        sp.wait_ge(x_ld[u], 16 * g)
                    if known and n == 0:
                        weights(0)
                    load_list(lg[u], lg_ld[u], n)
                    if not known or n >= 2:
                        weights(n - 1)
                    if not known or n >= LAG_S:
                        m = n - LAG_S
                        if not known or m >= UN:
                            sp.wait_ge(added[(u - LAG_S) % UN], 16 * (g - (1 if u >= LAG_S - UN else 2)))
                        load_list(ls[(u - LAG_S) % UN], ls_ld[(u - LAG_S) % UN], m)

                for n in range(3 * UN):
                    step(n // UN, n % UN)
                last_turn = field(sp, 0, 5, NTURN - 1)
                with sp.Fori(3, NTURN + 1) as g:
                    with sp.If(last_turn >= g - 1):
                        for u in range(UN):
                            step(g, u)
                assert LAG_S == UN + 1
                sp.wait_ge(added[UN - 1], 16 * last_turn)
                load_list(ls[UN - 1], ls_ld[UN - 1], UN * last_turn + UN - 1)

            @blk.gpsimd
            def _(pool):
                def gather(g, u):
                    pool.wait_ge(lg_ld[u], 16 * (g + 1))
                    pool.nop(nofuse=True)
                    nc.gpsimd.indirect_dma_start(xg[u][:], None, y_rows,
                                                 bass.IndirectOffsetOnAxis(ap=lg[u][:, 0:1].bitcast(U32), axis=0)).then_inc(x_ld[u], 16)

                def scatter(m, u, gm):
                    pool.wait_ge(act_do, m + 1)
                    pool.wait_ge(ls_ld[u], 16 * (gm + 1))
                    with pool.If(field(pool, m, 6, 1) > 0):
                        for d in range(1, UN + 1):
                            done = gm + 1 if d <= u else gm
                            if d < UN and some(done):
                                pool.wait_ge(added[(u - d) % UN], 16 * done)
                        if some(gm):
                            pool.wait_ge(added[u], 16 * gm)
                    pool.nop(nofuse=True)
                    nc.gpsimd.indirect_dma_start(out, bass.IndirectOffsetOnAxis(ap=ls[u][:, 0:1].bitcast(U32), axis=0),
                                                 og[u][:], None, compute_op=ALU.add).then_inc(added[u], 16)

                def step(g, u):
                    j = g * UN + u
                    pool.wait_ge(pe_x, j + 1)
                    gather(g + 1, u)
                    if not isinstance(j, int) or j >= 3:
                        scatter(j - 3, (u - 3) % UN, g - 1 if u < 3 else g)

                pool.wait_ge(tab_ld, 16)
                for u in range(UN):
                    gather(0, u)
                for u in range(UN):
                    step(0, u)
                for u in range(UN):
                    step(1, u)
                last_turn = field(pool, 0, 5, NTURN - 1)
                with pool.Fori(2, NTURN) as g:
                    with pool.If(last_turn >= g):
                        for u in range(UN):
                            step(g, u)
                for u in range(1, UN):
                    scatter(UN * last_turn + u, u, last_turn)
                for u in range(UN):
                    pool.wait_ge(x_ld[u], 16 * last_turn + 32)
                for u in range(UN):
                    pool.wait_ge(added[u], 16 * last_turn + 16)

            @blk.tensor
            def _(pe):
                pe.wait_ge(tab_ld, 16)
                pe.sem_inc(pe_do, 1)

                def turn_x(j, u, g):
                    pe.wait_ge(x_ld[u], 16 * (g + 1))
                    for k in range(KC):
                        last = nc.tensor.transpose(b_x[u % 2][:, k * P:(k + 1) * P].bitcast(F32R),
                                                   xg[u][:, k * P:(k + 1) * P].bitcast(F32R), ident_r[:])
                    last.then_inc(pe_x, 1)

                def gate_up(j, u, place):
                    pe.wait_ge(dve_x, j + 1)
                    for k in range(KC):
                        for a, b in ((0, 0), (0, 1), (1, 0)):
                            last = nc.tensor.matmul(b_gu[u % 2][:], xp[a][:, u % 2, k, :],
                                                    wgu[b][:, bass.ds(place, 1), k, :].rearrange("p a n -> p (a n)"),
                                                    start=(k == 0 and a == b == 0), stop=(k == KC - 1 and a == 1))
                    last.then_inc(pe_gu, 1)

                def turn_h(j, u):
                    pe.wait_ge(dve_gu, j + 1)
                    for k in range(KH):
                        last = nc.tensor.transpose(b_h[u % 2][:, k * P:(k + 1) * P], hf[:, u % 2, k * P:(k + 1) * P], ident[:])
                    last.then_inc(pe_ht, 1)

                def down(j, u, place):
                    if not isinstance(j, int) or j >= 2:
                        pe.wait_ge(act_do, j - 1)
                    pe.wait_ge(dve_ht, j + 1)
                    for k in range(KH):
                        for a, b in ((0, 0), (0, 1), (1, 0)):
                            last = nc.tensor.matmul(b_o[u % 2][:], hp[a][:, u % 2, k, :],
                                                    wdn[b][:, bass.ds(place, 1), k, :].rearrange("p a n -> p (a n)"),
                                                    start=(k == 0 and a == b == 0), stop=(k == KH - 1 and a == 1))
                    last.then_inc(pe_do, 1)

                def step(g, u, turn):
                    j = g * UN + u
                    turn_x(j + 1, (u + 1) % UN, g + 1 if u == UN - 1 else g)
                    place = turn.place(u)
                    pe.wait_ge(split, 3 * turn.order(u) + 3 + SPLIT_0)
                    gate_up(j, u, place)
                    if not isinstance(j, int) or j >= 1:
                        turn_h(j - 1, (u - 1) % UN)
                    if not isinstance(j, int) or j >= 2:
                        down(j - 2, (u - 2) % UN, turn.place(u - 2))

                pe.wait_ge(ident_ok, 1)
                pe.wait_ge(words, 1)
                turn_x(0, 0, 0)
                for g in range(2):
                    turn = Turn(pe, g)
                    for u in range(UN):
                        step(g, u, turn)
                last_turn = field(pe, 0, 5, NTURN - 1)
                with pe.Fori(2, NTURN) as g:
                    with pe.If(last_turn >= g):
                        turn = Turn(pe, g)
                        for u in range(UN):
                            step(g, u, turn)
                end = UN * last_turn + UN - 1
                turn_h(end, UN - 1)
                down(UN * last_turn + UN - 2, UN - 2, field(pe, UN * last_turn + UN - 2, 1, E) & (RING - 1))
                down(end, UN - 1, field(pe, end, 1, E) & (RING - 1))

            @blk.scalar
            def _(act):
                act.wait_ge(tab_ld, 16)

                def x_high(j, u):
                    act.wait_ge(pe_x, j + 1)
                    if not isinstance(j, int) or j >= 2:
                        act.wait_ge(pe_gu, j - 1)
                    nc.scalar.copy(xp[0][:, u % 2, :, :].rearrange("p k t -> p (k t)"), b_x[u % 2][:]).then_inc(act_x, 1)

                def silu(j, u):
                    act.wait_ge(pe_gu, j + 1)
                    if not isinstance(j, int) or j >= 2:
                        act.wait_ge(dve_gu, j - 1)
                    nc.scalar.activation(sg[:, u % 2, :], b_gu[u % 2][:, 0:H], ACT.Silu).then_inc(act_gu, 1)

                def h_high(j, u):
                    act.wait_ge(pe_ht, j + 1)
                    if not isinstance(j, int) or j >= 2:
                        act.wait_ge(pe_do, j)
                    nc.scalar.copy(hp[0][:, u % 2, :, :].rearrange("p k t -> p (k t)"), b_h[u % 2][:, 0:H]).then_inc(act_ht, 1)

                def weigh(j, u, g):
                    act.wait_ge(pe_do, j + 2)
                    act.wait_ge(ls_ld[u], 16 * (g + 1))
                    if not isinstance(j, int) or j >= UN:
                        act.wait_ge(added[u], 16 * g)
                    nc.scalar.activation(og[u][:], b_o[u % 2][:], ACT.Copy, scale=ls[u][:, 1:2].bitcast(F32)).then_inc(act_do, 1)

                def weights_high(order, half, place, part):
                    gu, k0, k1 = PARTS[part]
                    nc.scalar.copy((wgu if gu else wdn)[0][:, bass.ds(place, 1), k0:k1, :].rearrange("p a k n -> p (a k n)"),
                                   raw[0 if gu else 1][:, bass.ds(half, 1), k0:k1, :].rearrange("p a k n -> p (a k n)")
                                   ).then_inc(w_high, 1)

                def start_weights(j, order):
                    if j is not None:
                        act.wait_ge(pe_do, field(act, j, 4, MAXT) + 1)
                    act.wait_ge(raw_gu_ld, 32 * order + 32)
                    weights_high(order, order & 1, order & (RING - 1), 0)

                def end_weights(order):
                    weights_high(order, order & 1, order & (RING - 1), 1)
                    act.wait_ge(raw_d_ld, 16 * order + 16)
                    weights_high(order, order & 1, order & (RING - 1), 2)

                def step(g, u, turn):
                    j = g * UN + u
                    known = isinstance(j, int)
                    x_high(j + 1, (u + 1) % UN)
                    if not known or j >= 3:
                        weigh(j - 3, (u - 3) % UN, g - 1 if u < 3 else g)
                    with act.If(turn.first(u + 2) > 0):
                        start_weights(j + 2, turn.order(u + 2))
                    silu(j, u)
                    if not known or j >= 1:
                        h_high(j - 1, (u - 1) % UN)
                    with act.If(turn.first(u + 2) > 0):
                        end_weights(turn.order(u + 2))

                act.wait_ge(words, 1)
                start_weights(None, 0)
                end_weights(0)
                x_high(0, 0)
                turn = Turn(act, 0)
                with act.If(turn.first(1) > 0):
                    start_weights(None, turn.order(1))
                    end_weights(turn.order(1))
                for u in range(UN):
                    step(0, u, turn)
                turn = Turn(act, 1)
                for u in range(UN):
                    step(1, u, turn)
                last_turn = field(act, 0, 5, NTURN - 1)
                with act.Fori(2, NTURN) as g:
                    with act.If(last_turn >= g):
                        turn = Turn(act, g)
                        for u in range(UN):
                            step(g, u, turn)
                end = UN * last_turn + UN - 1
                weigh(UN * last_turn + UN - 3, UN - 3, last_turn)
                h_high(end, UN - 1)
                weigh(UN * last_turn + UN - 2, UN - 2, last_turn)
                weigh(end, UN - 1, last_turn)

            @blk.vector
            def _(dve):
                dve.wait_ge(tab_ld, 16)
                dve.sem_inc(split, SPLIT_0)
                nc.vector.tensor_copy(ident_r[:], ident[:]).then_inc(ident_ok, 1)

                def x_low(j, u):
                    dve.wait_ge(act_x, j + 1)
                    sub_exact(nc, xp[1][:, u % 2, :, :].rearrange("p k t -> p (k t)"), b_x[u % 2][:],
                              xp[0][:, u % 2, :, :].rearrange("p k t -> p (k t)")).then_inc(dve_x, 1)

                def hidden(j, u):
                    dve.wait_ge(act_gu, j + 1)
                    if not isinstance(j, int) or j >= 2:
                        dve.wait_ge(pe_ht, j - 1)
                    nc.vector.tensor_tensor(hf[:, u % 2, :], b_gu[u % 2][:, H:2 * H], sg[:, u % 2, :], ALU.mult).then_inc(dve_gu, 1)

                def h_low(j, u):
                    dve.wait_ge(act_ht, j + 1)
                    sub_exact(nc, hp[1][:, u % 2, :, :].rearrange("p k t -> p (k t)"), b_h[u % 2][:, 0:H],
                              hp[0][:, u % 2, :, :].rearrange("p k t -> p (k t)")).then_inc(dve_ht, 1)

                def weights_low(order, parts):
                    half, place = order & 1, order & (RING - 1)
                    dve.wait_ge(w_high, 3 * order + parts[-1] + 1)
                    for part in parts:
                        gu, k0, k1 = PARTS[part]
                        w = wgu if gu else wdn
                        sub_exact(nc, w[1][:, bass.ds(place, 1), k0:k1, :].rearrange("p a k n -> p (a k n)"),
                                  raw[0 if gu else 1][:, bass.ds(half, 1), k0:k1, :].rearrange("p a k n -> p (a k n)"),
                                  w[0][:, bass.ds(place, 1), k0:k1, :].rearrange("p a k n -> p (a k n)")).then_inc(split, 1)

                def step(g, u, turn):
                    j = g * UN + u
                    x_low(j + 1, (u + 1) % UN)
                    with dve.If(turn.first(u + 1) > 0):
                        weights_low(turn.order(u + 1), (1, 2))
                    hidden(j, u)
                    if not isinstance(j, int) or j >= 1:
                        h_low(j - 1, (u - 1) % UN)
                    with dve.If(turn.first(u + 2) > 0):
                        weights_low(turn.order(u + 2), (0,))

                def of_turns(b, f):
                    return trow[0:1, b * FLD + f:(b + (NWORD - 1) * UN) * FLD + f + 1:UN * FLD]

                n_link = [0]

                def link(ins):
                    n_link[0] += 1
                    ins.then_inc(words_chain, 1)
                    dve.wait_ge(words_chain, n_link[0])

                link(nc.vector.tensor_copy(turns[:], of_turns(FIRSTS - 2, 3)))
                for b in range(FIRSTS - 3, -1, -1):
                    link(nc.vector.scalar_tensor_tensor(out=turns[:], in0=turns[:], scalar=2.0, in1=of_turns(b, 3),
                                                        op0=ALU.mult, op1=ALU.add))
                link(nc.vector.tensor_scalar(turns[:], turns[:], 2.0, None, ALU.mult))
                link(nc.vector.tensor_tensor(turns[0:1, 1:NWORD], turns[0:1, 1:NWORD], of_turns(UN - 1, 3)[:, 0:NWORD - 1],
                                             ALU.add))
                nc.vector.scalar_tensor_tensor(out=turns[:], in0=of_turns(0, 1), scalar=float(1 << FIRSTS), in1=turns[:],
                                               op0=ALU.mult, op1=ALU.add).then_inc(words, 1)
                dve.wait_ge(words, 1)
                weights_low(0, (0, 1, 2))
                x_low(0, 0)
                turn = Turn(dve, 0)
                with dve.If(turn.first(1) > 0):
                    weights_low(turn.order(1), (0,))
                for u in range(UN):
                    step(0, u, turn)
                turn = Turn(dve, 1)
                for u in range(UN):
                    step(1, u, turn)
                last_turn = field(dve, 0, 5, NTURN - 1)
                with dve.Fori(2, NTURN) as g:
                    with dve.If(last_turn >= g):
                        turn = Turn(dve, g)
                        for u in range(UN):
                            step(g, u, turn)
                h_low(UN * last_turn + UN - 1, UN - 1)


_INS = ['x', 'cond_512', 'L0_cond_weight', 'L0_cond_bias', 'L0_cond_affine_w', 'L0_cond_affine_b', 'L0_ffn_router_w',
        'L0_ffn_e_bias', 'L0_ffn_gate_w', 'L0_ffn_up_w', 'L0_ffn_down_w', 'L0_ffn_sh_gate_w', 'L0_ffn_sh_up_w',
        'L0_ffn_sh_down_w']
_OUTS = [((8 * 1024 + P, 512), 'float32')]


def kernel(**inputs):
    import numpy as _np
    import concourse.bacc as _bacc
    from concourse import mybir as _mybir
    from concourse.bass_utils import run_bass_kernel_spmd as _run

    nc = _bacc.Bacc("TRN2", target_bir_lowering=False, num_devices=1)
    arrays, args = {}, []
    for name in _INS:
        a = _np.ascontiguousarray(inputs[name])
        arrays[f"in_{name}_dram"] = a
        args.append(nc.dram_tensor(f"in_{name}_dram", a.shape, _mybir.dt.from_np(a.dtype), kind="ExternalInput").ap())
    for i, (shape, dtype) in enumerate(_OUTS):
        dt = _mybir.dt.from_np(_np.dtype(dtype))
        args.append(nc.dram_tensor(f"out_{i}_dram", shape, dt, kind="ExternalOutput").ap())
    build(nc, *args)
    r = _run(nc, [arrays], core_ids=[0])
    got = tuple(r.results[0][f"out_{i}_dram"] for i in range(len(_OUTS)))
    return got[0][:8 * 1024].reshape(8, 1024, 512)
```
